# Optimizing a Trainium2 kernel written in Bass

```python
import numpy as np
import jax
import jax.numpy as jnp

def _softmax(x, axis=-1):
    return jax.nn.softmax(x, axis=axis)

def _gelu(x):
    return jax.nn.gelu(x, approximate=True)

def _silu(x):
    return jax.nn.silu(x)

def _sigmoid(x):
    return jax.nn.sigmoid(x)

def _layernorm(x, axis=-1, eps=1e-05):
    m = jnp.mean(x, axis=axis, keepdims=True)
    v = jnp.var(x, axis=axis, keepdims=True)
    return (x - m) / jnp.sqrt(v + eps)

def _scatter_add(tgt, idx, src, axis=0):
    return tgt.at[idx].add(src)

def _segment_sum(src, seg, n):
    return jax.ops.segment_sum(src, seg, n)
kernel_name = 'mk_adj_preln_d1_adj_r2_1bcdfb'

def setup_inputs(seed: int=0):
    np.random.seed(seed)
    _w = jnp.asarray

    def _rec_inputs():
        import jax
        import jax.numpy as jnp
        _gk = jax.random.key(seed)
        x = 7.22e-05 + 1 * jax.random.normal(jax.random.fold_in(_gk, 1), (64, 128, 1024), jnp.float32)
        _a = jax.random.bernoulli(jax.random.fold_in(_gk, 2), 0.015625, (128, 128))
        _a = jnp.logical_or(_a, jnp.swapaxes(_a, -1, -2))
        _a = jnp.logical_or(_a, jnp.eye(128, dtype=bool))
        _af = _a.astype(jnp.float32)
        _af = _af * jax.random.uniform(jax.random.fold_in(_gk, 3), (128, 128), jnp.float32, 0.05, 0.27663)
        adj = _af
        return (x, adj)
    x, adj = _rec_inputs()

    def _L0_gnn_setup():
        import jax, jax.numpy as jnp
        import numpy as np
        N, B, T = (1024, 16, 128)
        key = jax.random.key(seed)
        k1, k2, k3, k4 = jax.random.split(key, 4)
        x = jax.random.normal(k1, (B, T, N), dtype=jnp.float32)
        weight = jax.random.normal(k2, (T, T), dtype=jnp.float32) * (1.0 / np.sqrt(T))
        bias = jax.random.normal(k3, (T,), dtype=jnp.float32) * 0.01
        u = jax.random.uniform(k4, (N * N, 2), dtype=jnp.float32, minval=1e-06, maxval=1.0 - 1e-06)
        gumbel = -jnp.log(-jnp.log(u))
        return {'x': x, 'weight': weight, 'bias': bias, 'gumbel': gumbel}
    _L0_gnn_all = _L0_gnn_setup()
    _L0_gnn_in = {k: v for k, v in _L0_gnn_all.items() if k in ('bias', 'gumbel')}
    del _L0_gnn_all
    return {'x': x, 'adj': adj, 'L0_gnn_bias': _L0_gnn_in['bias'], 'L0_gnn_gumbel': _L0_gnn_in['gumbel']}

def reference(x, adj, L0_gnn_bias, L0_gnn_gumbel):
    import jax
    import jax.numpy as jnp

    def _L0_gnn_ref(x, weight, bias, gumbel):
        import jax, jax.numpy as jnp
        import numpy as np
        N, B, T = (1024, 16, 128)
        xp = jnp.transpose(x, (2, 0, 1))
        n = xp.shape[0]
        xs = jax.lax.stop_gradient(xp)
        x_avg = xs.mean(axis=1)
        x_norm = x_avg / jnp.maximum(jnp.linalg.norm(x_avg, axis=-1, keepdims=True), 1e-12)
        sim = (x_norm @ x_norm.T + 1.0) * 0.5
        sim_flat = sim.reshape(-1)
        score0 = sim_flat + gumbel[:, 0]
        score1 = 1.0 - sim_flat + gumbel[:, 1]
        adj = (score0 > score1).astype(xp.dtype).reshape(n, n)
        adj_sym = jnp.clip(adj + adj.T, 0.0, 1.0)
        nmask = jnp.clip(adj_sym + jnp.eye(n, dtype=xp.dtype), 0.0, 1.0)
        common = nmask @ nmask.T
        max_common = common.max()
        valid = adj_sym * (common > 1.0).astype(xp.dtype) > 0
        struct = jnp.where(valid, common / max_common * common, 0.0)
        W = adj * struct
        deg = W.sum(axis=0)
        dinv = jnp.where(deg > 0, deg ** (-0.5), 0.0)
        Wn = dinv[:, None] * W * dinv[None, :]
        xw = jnp.einsum('nbt,to->nbo', xp, weight)
        out = jnp.einsum('sd,sbt->dbt', Wn, xw) + bias
        return jnp.transpose(out, (1, 2, 0))
    h = jnp.maximum(_layernorm(x, axis=-1), 0.0)
    x = x + _L0_gnn_ref(h, adj, L0_gnn_bias, L0_gnn_gumbel)
    return x

_drawn_inputs = setup_inputs


def setup_inputs(seed=0):
    import zlib

    import numpy as np

    out = dict(_drawn_inputs(seed))
    spreads = {}
    factors = {'L0_gnn_bias': 6.086, 'L0_gnn_gumbel': 8.0}
    for name, (base, spread) in spreads.items():
        noise = np.random.default_rng([zlib.crc32(name.encode()), seed]).standard_normal(out[name].shape)
        drawn = base * np.exp(spread * noise) if base else spread * noise
        out[name] = jnp.asarray(drawn.astype(out[name].dtype))
    for name, factor in factors.items():
        out[name] = (out[name] * factor).astype(out[name].dtype)
    return out
```

```python
from contextlib import ExitStack

import concourse.bass as bass
from concourse import mybir


def bass_preln_graph_layer(
    nc: bass.Bass,
    x: bass.AP,
    adj: bass.AP,
    bias: bass.AP,
    gumbel: bass.AP,
    out: bass.AP,
):
    fp32 = mybir.dt.float32
    fp16 = mybir.dt.float16
    int32 = mybir.dt.int32
    ALU = mybir.AluOpType
    ACT = mybir.ActivationFunctionType
    AX = mybir.AxisListType

    B, T, N = x.shape
    P = 128
    NB = N // P
    HALF = 512
    GROUPS = B // 4
    STREAMED = 3
    LN_EPS = 1e-5
    NORM_EPS = 1e-12
    W_TOP = 2.0 ** 9
    B_TOP = 2.0 ** 14
    TINY = 1e-18
    EXPONENT = 0x7F800000

    def entry(g, k):
        return g if k == STREAMED else GROUPS + STREAMED * g + k

    gumbel_block = gumbel.rearrange("(i p j) c -> i p (j c)", p=P, j=N)

    ctx = ExitStack()
    with ctx:
        def sb(name, shape, dt=fp32):
            return ctx.enter_context(nc.sbuf_tensor(name, shape, dt))

        def sem(name):
            return ctx.enter_context(nc.semaphore(name))

        cache = sb("cache", [P, GROUPS * 2 * N], fp16)
        xw_u = sb("xw_u", [P, STREAMED, 2, N], fp16)
        xring = sb("xring", [P, 8, N])
        region_a = sb("region_a", [P, 8, N])
        hring = sb("hring", [P, STREAMED, N])
        adj_m = sb("adj_m", [P, NB, N], fp16)
        nm_m = sb("nm_m", [P, NB, N], fp16)
        gout = sb("gout", [P, 4, N])
        rs_row = sb("rs_row", [P, N])

        adj_f = adj_m[:, :, :].rearrange("p a n -> p (a n)").bitcast(fp32)
        nm_f = nm_m[:, :, :].rearrange("p a n -> p (a n)").bitcast(fp32)
        b_hi, b_lo = nm_m, adj_m
        a_m = region_a

        x1 = [xring[:, s, :] for s in range(8)] + [region_a[:, s, :] for s in range(8)]
        h1 = [hring[:, s, :] for s in range(3)] + [adj_f[:, s * N:(s + 1) * N] for s in range(4)] + [nm_f[:, 0:N]]
        pool_sum = nm_f[:, N:2 * N]
        goutf = gout[:, :, :].rearrange("p a n -> p (a n)")
        gum = [goutf[:, 0:2 * N], goutf[:, 2 * N:4 * N], nm_f[:, 2 * N:4 * N], nm_f[:, 0:2 * N]]
        sim_h = [region_a[:, s, :] for s in (0, 1)]
        one_m = [region_a[:, s, :] for s in (2, 3)]
        score0 = [region_a[:, s, :] for s in (4, 5)]
        score1 = [region_a[:, s, :] for s in (6, 7)]
        x_sum = xring[:, 4, :]
        x_nrm = xring[:, 5, :]
        x_sq = xring[:, 6, :]
        diag_c = xring[:, 7, :]
        diag_r = xring[:, 6, :]
        c_row = xring[:, 4, :]

        w_in = gout[:, 3, 0:P]
        w_t = gout[:, 3, P:2 * P]
        w_s = sb("w_s", [P, P])
        ident = sb("ident", [P, P])
        ident16 = sb("ident16", [P, P], fp16)
        ones = sb("ones", [P, P])
        bias_c = sb("bias_c", [P, 1])
        l1 = sb("l1", [P, 1])
        w_pow = sb("w_pow", [P, 1])
        w_up = sb("w_up", [P, 1])
        w_back = sb("w_back", [P, 1])
        stats = sb("stats", [P, 2, 4, 2, 6])
        mv = sb("mv", [P, 2, 4, 2])
        ve4 = sb("ve4", [P, 2, 4])
        sd = sb("sd", [P, 2, 4])
        y0 = sb("y0", [P, 2, 4])
        nt = sb("nt", [P, 2, 4])
        rstd = sb("rstd", [P, 2, 4])
        nmr = sb("nmr", [P, 2, 4])
        threes = sb("threes", [P, 4])
        zeros = sb("zeros", [P, 4])
        wait_pad = sb("wait_pad", [P, 1])
        col_v = sb("col_v", [P, NB])
        col_s = sb("col_s", [P, NB])
        col_y = sb("col_y", [P, NB])
        col_t = sb("col_t", [P, NB])
        rnorm = sb("rnorm", [P, NB])
        dinv = sb("dinv", [P, NB])
        s_col = sb("s_col", [P, NB])
        c_col = sb("c_col", [P, NB])
        r_col = sb("r_col", [P, NB])

        psum = ctx.enter_context(nc.psum_tensor("psum", [P, 8 * HALF], fp32))
        big = [psum[:, 0:N], psum[:, N:2 * N]]
        xwp = [psum[:, 2 * N:3 * N], psum[:, 3 * N:4 * N]]
        sum_ps = big[0]
        wt_ps = big[1][:, 0:P]
        ws_ps = big[1][:, HALF:HALF + P]
        norm_ps = xwp[0][:, 0:NB]
        deg_ps = xwp[0][:, 0:NB]
        s_ps = xwp[0][:, HALF:HALF + NB]

        consts = sem("consts")
        w_loaded = sem("w_loaded")
        bias_loaded = sem("bias_loaded")
        w_turned = sem("w_turned")
        w_scaled = sem("w_scaled")
        w_back_turned = sem("w_back_turned")
        w_ready = sem("w_ready")
        x_loaded = [sem(f"x_loaded{s}") for s in range(16)]
        g_loaded = [sem(f"g_loaded{s}") for s in range(4)]
        dve_step = sem("dve_step")
        pool_step = sem("pool_step")
        stats_made = sem("stats_made")
        mv_made = sem("mv_made")
        ve_made = sem("ve_made")
        sd_made = sem("sd_made")
        y0_made = sem("y0_made")
        rstd_made = sem("rstd_made")
        h_made = sem("h_made")
        h_used = sem("h_used")
        pool_added = sem("pool_added")
        xw_done = sem("xw_done")
        hi_made = sem("hi_made")
        lo_made = sem("lo_made")
        xsum_made = sem("xsum_made")
        sq_made = sem("sq_made")
        norm_done = sem("norm_done")
        normv_made = sem("normv_made")
        norms_made = sem("norms_made")
        diagn_made = sem("diagn_made")
        rnrow_done = sem("rnrow_done")
        xnrm_made = sem("xnrm_made")
        sim_done = sem("sim_done")
        simh_made = sem("simh_made")
        onem_made = sem("onem_made")
        score0_made = sem("score0_made")
        score1_made = sem("score1_made")
        adj_made = sem("adj_made")
        sym_done = sem("sym_done")
        nm_even = sem("nm_even")
        nm_odd = sem("nm_odd")
        common_done = sem("common_done")
        sq_common = sem("sq_common")
        more_than_one = sem("more_than_one")
        a_made = sem("a_made")
        deg_done = sem("deg_done")
        degv_made = sem("degv_made")
        degs_made = sem("degs_made")
        dinv_made = sem("dinv_made")
        s_done = sem("s_done")
        diagc_made = sem("diagc_made")
        diagr_made = sem("diagr_made")
        rcol_made = sem("rcol_made")
        crow_done = sem("crow_done")
        rrow_done = sem("rrow_done")
        crow_made = sem("crow_made")
        rrow_made = sem("rrow_made")
        b_made = sem("b_made")
        bhi_made = sem("bhi_made")
        blo_dve = sem("blo_dve")
        blo_pool = sem("blo_pool")
        p_stats = sem("p_stats")
        p_mv = sem("p_mv")
        p_ve = sem("p_ve")
        p_sd = sem("p_sd")
        p_y0 = sem("p_y0")
        p_rstd = sem("p_rstd")
        p_h = sem("p_h")
        p_xw = sem("p_xw")
        p_hi = sem("p_hi")
        p_lo = sem("p_lo")
        main_done = sem("main_done")
        scaled = sem("scaled")
        out_made = sem("out_made")
        out_stored = [sem(f"out_stored{s}") for s in range(4)]

        block = ctx.enter_context(nc.Block())

        def cached_xw(g, part):
            at = (g * 2 + part) * N
            return cache[:, bass.ds(at, N)]

        @block.sync
        def _(sp):
            def load_x(slot, g, k):
                sp.dma_start(x1[slot], x[entry(g, k), :, :]).then_inc(x_loaded[slot], 16)

            def load_gumbel(i):
                sp.dma_start(gum[i % 4], gumbel_block[i, :, :]).then_inc(g_loaded[i % 4], 16)

            load_x(0, 0, 0)
            load_x(1, 0, 1)
            sp.dma_start(w_in, adj).then_inc(w_loaded, 16)
            for s in range(2, 16):
                load_x(s, s // 4, s % 4)
            sp.dma_start(bias_c[:, :], bias.rearrange("(p a) -> p a", a=1)).then_inc(bias_loaded, 16)
            with sp.Fori(1, GROUPS // 4) as it:
                for s in range(16):
                    sp.wait_ge(h_made, it * 16 + (s - 15))
                    load_x(s, it * 4 + s // 4, s % 4)

            for i in range(3):
                load_gumbel(i)
            for s in range(STREAMED):
                sp.wait_ge(h_made, 4 * GROUPS - 15 + s)
            sp.wait_ge(xsum_made, 1)
            load_gumbel(3)
            for i in range(4, NB):
                sp.wait_ge(adj_made, i - 3)
                load_gumbel(i)
            for s in range(4):
                load_x(s, 0, s)
            sp.wait_ge(b_made, NB)
            sp.wait_ge(rrow_done, 1)
            for s in range(4, 8):
                load_x(s, 1, s - 4)

            def store(g, k):
                sp.wait_ge(out_made, 4 * g + (k + 1))
                sp.dma_start(out[entry(g, k), :, :], gout[:, k, :]).then_inc(out_stored[k], 16)

            with sp.Fori(0, GROUPS // 2 - 1) as it:
                for s in range(8):
                    store(it * 2 + s // 4, s % 4)
                    load_x(s, it * 2 + (s // 4 + 2), s % 4)
            for s in range(8):
                store(GROUPS - 2 + s // 4, s % 4)
            for k in range(4):
                sp.wait_ge(out_stored[k], 16 * GROUPS)

        @block.gpsimd
        def _(pool):
            step = [0]

            def link(ins):
                step[0] += 1
                ins.then_inc(pool_step, 1)
                pool.wait_ge(pool_step, step[0])

            link(nc.gpsimd.memset(ident[:, :], 0.0))
            link(nc.gpsimd.affine_select(out=ident[:, :], in_=ident[:, :], compare_op=ALU.not_equal, fill=1.0,
                                         base=0, pattern=[[-1, P]], channel_multiplier=1))
            nc.gpsimd.tensor_copy(ident16[:, :], ident[:, :]).then_inc(consts, 1)
            nc.gpsimd.memset(ones[:, :], 1.0).then_inc(consts, 1)
            link(nc.gpsimd.memset(threes[:, :], 3.0))
            link(nc.gpsimd.memset(zeros[:, :], 0.0))
            nc.gpsimd.memset(pool_sum, 0.0).then_inc(pool_added, 1)

            def newton(q, kk, y_ready, count, signal, base):
                pool.wait_ge(y_ready, count)
                y, v, t, r, m = y0[:, q, 0:kk], ve4[:, q, 0:kk], nt[:, q, 0:kk], rstd[:, q, 0:kk], nmr[:, q, 0:kk]
                nc.gpsimd.tensor_tensor(t, y, y, ALU.mult).then_inc(pool_step, 1)
                pool.wait_ge(pool_step, base + 1)
                nc.gpsimd.tensor_tensor(t, t, v, ALU.mult).then_inc(pool_step, 1)
                pool.wait_ge(pool_step, base + 2)
                nc.gpsimd.tensor_tensor(t, threes[:, 0:kk], t, ALU.subtract).then_inc(pool_step, 1)
                pool.wait_ge(pool_step, base + 3)
                nc.gpsimd.tensor_tensor(r, y, t, ALU.mult).then_inc(pool_step, 1)
                pool.wait_ge(pool_step, base + 4)
                nc.gpsimd.tensor_tensor(m, mv[:, q, 0:kk, 0], r, ALU.mult).then_inc(pool_step, 1)
                pool.wait_ge(pool_step, base + 5)
                nc.gpsimd.tensor_tensor(m, zeros[:, 0:kk], m, ALU.subtract).then_inc(signal, 1)

            base1 = step[0]
            with pool.Fori(0, GROUPS // 4) as it:
                for u in range(4):
                    newton(u % 2, 4, y0_made, it * 4 + (u + 1), rstd_made, it * 20 + (base1 + 5 * u))
                    for k in range(2):
                        pool.wait_ge(h_made, it * 16 + (4 * u + k + 1))
                        pool.wait_ge(pool_added, it * 8 + (2 * u + k + 1))
                        nc.gpsimd.tensor_tensor(pool_sum, pool_sum, h1[(4 * u + k) % 8],
                                                ALU.add).then_inc(pool_added, 1)

            for i in range(NB):
                pool.wait_ge(onem_made, i + 1)
                pool.wait_ge(g_loaded[i % 4], 16 * (i // 4 + 1))
                if i >= 2:
                    pool.wait_ge(adj_made, i - 1)
                nc.gpsimd.tensor_tensor(score1[i % 2], one_m[i % 2], gum[i % 4][:, 1:2 * N:2],
                                        ALU.add).then_inc(score1_made, 1)

            base2 = base1 + 5 * GROUPS
            newton(0, STREAMED, p_y0, 1, p_rstd, base2)
            pool.wait_ge(rcol_made, 1)
            for j in range(NB):
                last = nc.gpsimd.tensor_scalar(diag_r[:, j * P:(j + 1) * P], ident[:, :], r_col[:, j:j + 1], None,
                                               ALU.mult)
            last.then_inc(diagr_made, 1)
            for i in range(0, NB, 2):
                pool.wait_ge(bhi_made, i + 1)
                nc.gpsimd.tensor_tensor(b_lo[:, i, :], a_m[:, i, :], b_hi[:, i, :],
                                        ALU.subtract).then_inc(blo_pool, 1)

            with pool.Fori(1, GROUPS) as g:
                newton(0, STREAMED, p_y0, g + 1, p_rstd, g * 5 + base2)

        @block.scalar
        def _(act):
            def normalise(x_tile, h_tile, q, k, signal):
                nc.scalar.activation(h_tile, x_tile, ACT.Relu, bias=nmr[:, q, k:k + 1],
                                     scale=rstd[:, q, k:k + 1]).then_inc(signal, 1)

            def root(q, kk, signal):
                nc.scalar.activation(sd[:, q, 0:kk], ve4[:, q, 0:kk], ACT.Sqrt).then_inc(signal, 1)

            def hi_cached(g, u):
                act.wait_ge(xw_done, g + 1)
                nc.scalar.activation(cached_xw(g, 0), xwp[u], ACT.Copy).then_inc(hi_made, 1)

            act.wait_ge(ve_made, 1)
            root(0, 4, sd_made)

            def pass1(it, first, last):
                for u in range(4):
                    g = it * 4 + u
                    act.wait_ge(rstd_made, g + 1)
                    for k in range(4):
                        if not (first and u < 2):
                            if k < 2:
                                act.wait_ge(pool_added, g * 2 + (k - 2))
                            else:
                                act.wait_ge(h_used, g * 2 + (k - 5))
                        normalise(x1[4 * u + k], h1[(4 * u + k) % 8], u % 2, k, h_made)
                    if not (last and u == 3):
                        act.wait_ge(ve_made, g + 2)
                        root((u + 1) % 2, 4, sd_made)
                    if not (first and u == 0):
                        hi_cached(g - 1, (u + 1) % 2)

            pass1(0, True, False)
            with act.Fori(1, GROUPS // 4 - 1) as it:
                pass1(it, False, False)
            pass1(GROUPS // 4 - 1, False, True)
            hi_cached(GROUPS - 1, 1)

            act.wait_ge(xsum_made, 1)
            nc.scalar.activation(x_sq, x_sum, ACT.Square).then_inc(sq_made, 1)
            act.wait_ge(normv_made, 1)
            nc.scalar.activation(col_s[:, :], col_v[:, :], ACT.Sqrt).then_inc(norms_made, 1)

            for i in range(NB):
                act.wait_ge(sim_done, i + 1)
                if i >= 2:
                    act.wait_ge(score0_made, i - 1)
                nc.scalar.activation(sim_h[i % 2], big[i % 2], ACT.Copy, scale=0.5, bias=0.5).then_inc(simh_made, 1)
                act.wait_ge(simh_made, i + 1)
                if i >= 2:
                    act.wait_ge(score1_made, i - 1)
                nc.scalar.activation(one_m[i % 2], sim_h[i % 2], ACT.Copy, scale=-1.0, bias=1.0).then_inc(onem_made, 1)

            for i in range(0, NB, 2):
                act.wait_ge(sym_done, i + 1)
                nc.scalar.activation(nm_m[:, i, :], big[i % 2], ACT.Sign).then_inc(nm_even, 1)

            act.wait_ge(p_ve, 1)
            root(0, STREAMED, p_sd)
            for i in range(NB):
                act.wait_ge(common_done, i + 1)
                nc.scalar.activation(a_m[:, i, :], big[i % 2], ACT.Square).then_inc(sq_common, 1)
                if i < STREAMED:
                    if i == 0:
                        act.wait_ge(p_rstd, 1)
                    normalise(x1[i], h1[i], 0, i, p_h)

            def hi_streamed(n, k):
                act.wait_ge(p_xw, n + 1)
                nc.scalar.activation(xw_u[:, k, 0, :], xwp[1], ACT.Copy).then_inc(p_hi, 1)

            hi_streamed(0, 0)
            act.wait_ge(degv_made, 1)
            nc.scalar.activation(col_s[:, :], col_v[:, :], ACT.Sqrt).then_inc(degs_made, 1)
            act.wait_ge(crow_done, 1)
            nc.scalar.activation(c_row, big[0], ACT.Copy).then_inc(crow_made, 1)
            act.wait_ge(rrow_done, 1)
            nc.scalar.activation(rs_row[:, :], big[1], ACT.Copy).then_inc(rrow_made, 1)
            for i in range(NB):
                act.wait_ge(b_made, i + 1)
                nc.scalar.activation(b_hi[:, i, :], a_m[:, i, :], ACT.Copy).then_inc(bhi_made, 1)
            hi_streamed(1, 1)
            hi_streamed(2, 2)

            def pass2(it, us):
                for u in us:
                    g = it * 2 + u
                    act.wait_ge(p_ve, g + 2)
                    root(0, STREAMED, p_sd)
                    act.wait_ge(p_rstd, g + 2)
                    for k in range(STREAMED):
                        act.wait_ge(p_xw, g * 3 + (k + 1))
                        normalise(x1[4 * ((u + 1) % 2) + k], h1[k], 0, k, p_h)
                    for k in range(STREAMED):
                        act.wait_ge(main_done, g * 4 + (k + 1))
                        hi_streamed(g * 3 + (k + 3), k)

            with act.Fori(0, GROUPS // 2 - 1) as it:
                pass2(it, (0, 1))
            pass2(GROUPS // 2 - 1, (0,))

        @block.vector
        def _(dve):
            step = [0]

            def link(ins):
                step[0] += 1
                ins.then_inc(dve_step, 1)
                dve.wait_ge(dve_step, step[0])

            def moments(x_tile, q, k, signal):
                nc.vector.bn_stats(stats[:, q, k, 0, :], x_tile[:, 0:HALF])
                nc.vector.bn_stats(stats[:, q, k, 1, :], x_tile[:, HALF:N]).then_inc(signal, 1)

            def variance(q, kk, stats_sem, n_stats, mv_sem, n_mv, ve_sem):
                dve.wait_ge(stats_sem, n_stats)
                nc.vector.memset(wait_pad[:, :], 0.0)
                for k in range(kk):
                    last = nc.vector.bn_aggr(mv[:, q, k, :], stats[:, q, k, :, :])
                last.then_inc(mv_sem, 1)
                dve.wait_ge(mv_sem, n_mv)
                nc.vector.tensor_scalar(ve4[:, q, 0:kk], mv[:, q, 0:kk, 1], LN_EPS, 4.0, ALU.add,
                                        ALU.mult).then_inc(ve_sem, 1)

            def lo_cached(g, u):
                dve.wait_ge(hi_made, g + 1)
                nc.vector.tensor_tensor(cached_xw(g, 1), xwp[u], cached_xw(g, 0), ALU.subtract).then_inc(lo_made, 1)

            dve.wait_ge(w_turned, 1)
            link(nc.vector.tensor_reduce(l1[:, :], wt_ps, AX.X, ALU.add, apply_absolute_value=True))
            link(nc.vector.tensor_scalar(l1[:, :], l1[:, :], 1e-30, None, ALU.max))
            link(nc.vector.tensor_scalar(w_pow[:, :].bitcast(int32), l1[:, :].bitcast(int32), EXPONENT, None,
                                         ALU.bitwise_and))
            link(nc.vector.reciprocal(w_up[:, :], w_pow[:, :]))
            link(nc.vector.tensor_scalar(w_up[:, :], w_up[:, :], W_TOP, None, ALU.mult))
            link(nc.vector.tensor_scalar(w_back[:, :], w_pow[:, :], 1.0 / W_TOP, None, ALU.mult))
            nc.vector.tensor_scalar(w_t, wt_ps, w_up[:, 0:1], None, ALU.mult).then_inc(w_scaled, 1)
            dve.wait_ge(w_back_turned, 1)
            nc.vector.tensor_copy(w_s[:, :], ws_ps).then_inc(w_ready, 1)

            def tile_moments(it, u, k):
                dve.wait_ge(x_loaded[4 * u + k], it * 16 + 16)
                moments(x1[4 * u + k], u % 2, k, stats_made)

            for k in range(4):
                tile_moments(0, 0, k)
            variance(0, 4, stats_made, 4, mv_made, 1, ve_made)

            def pass1(it, first, last):
                for u in range(4):
                    g = it * 4 + u
                    more = not (last and u == 3)
                    nxt = (it, u + 1) if u < 3 else (it + 1, 0)
                    if more:
                        tile_moments(*nxt, 0)
                    dve.wait_ge(sd_made, g + 1)
                    nc.vector.reciprocal(y0[:, u % 2, :], sd[:, u % 2, :]).then_inc(y0_made, 1)
                    if more:
                        for k in range(1, 4):
                            tile_moments(*nxt, k)
                        variance((u + 1) % 2, 4, stats_made, g * 4 + 8, mv_made, g + 2, ve_made)
                    if not (first and u < 2):
                        lo_cached(g - 2, u % 2)

            pass1(0, True, False)
            with dve.Fori(1, GROUPS // 4 - 1) as it:
                pass1(it, False, False)
            pass1(GROUPS // 4 - 1, False, True)
            lo_cached(GROUPS - 2, 0)
            lo_cached(GROUPS - 1, 1)

            dve.wait_ge(h_used, 2 * GROUPS)
            dve.wait_ge(pool_added, 2 * GROUPS + 1)
            nc.vector.tensor_tensor(x_sum, sum_ps, pool_sum, ALU.add).then_inc(xsum_made, 1)

            def refine(v, y):
                link(nc.vector.tensor_tensor(col_t[:, :], y, y, ALU.mult))
                link(nc.vector.tensor_tensor(col_t[:, :], col_t[:, :], v, ALU.mult))
                link(nc.vector.tensor_scalar(col_t[:, :], col_t[:, :], -0.5, 1.5, ALU.mult, ALU.add))
                link(nc.vector.tensor_tensor(y, y, col_t[:, :], ALU.mult))

            dve.wait_ge(norm_done, 1)
            nc.vector.tensor_copy(col_v[:, :], norm_ps).then_inc(normv_made, 1)
            dve.wait_ge(norms_made, 1)
            link(nc.vector.tensor_scalar(col_y[:, :], col_s[:, :], TINY, None, ALU.max))
            link(nc.vector.reciprocal(rnorm[:, :], col_y[:, :]))
            dve.wait_ge(normv_made, 1)
            refine(col_v[:, :], rnorm[:, :])
            link(nc.vector.tensor_scalar(rnorm[:, :], rnorm[:, :], 1.0 / (B * NORM_EPS), None, ALU.min))
            for j in range(NB):
                last = nc.vector.tensor_scalar(diag_c[:, j * P:(j + 1) * P], ident[:, :], rnorm[:, j:j + 1], None,
                                               ALU.mult)
            last.then_inc(diagn_made, 1)
            dve.wait_ge(rnrow_done, 1)
            dve.wait_ge(xsum_made, 1)
            nc.vector.tensor_tensor(x_nrm, x_sum, xwp[1], ALU.mult).then_inc(xnrm_made, 1)

            def make_score0(i):
                dve.wait_ge(simh_made, i + 1)
                dve.wait_ge(g_loaded[i % 4], 16 * (i // 4 + 1))
                if i >= 2:
                    dve.wait_ge(adj_made, i - 1)
                nc.vector.tensor_tensor(score0[i % 2], sim_h[i % 2], gum[i % 4][:, 0:2 * N:2],
                                        ALU.add).then_inc(score0_made, 1)

            make_score0(0)
            for i in range(NB):
                if i + 1 < NB:
                    make_score0(i + 1)
                dve.wait_ge(score1_made, i + 1)
                dve.wait_ge(score0_made, i + 1)
                nc.vector.tensor_tensor(adj_m[:, i, :], score0[i % 2], score1[i % 2], ALU.is_gt).then_inc(adj_made, 1)

            for i in range(1, NB, 2):
                dve.wait_ge(sym_done, i + 1)
                nc.vector.tensor_scalar(nm_m[:, i, :], big[i % 2], 1.0, None, ALU.min).then_inc(nm_odd, 1)

            LOADS1 = 16 * (GROUPS // 4)

            def streamed_moments(q, nth, k, signal):
                dve.wait_ge(x_loaded[4 * q + k], nth * 16 + (LOADS1 + 16))
                moments(x1[4 * q + k], 0, k, signal)

            for k in range(STREAMED):
                streamed_moments(0, 0, k, p_stats)
            variance(0, STREAMED, p_stats, STREAMED, p_mv, 1, p_ve)
            dve.wait_ge(p_sd, 1)
            nc.vector.reciprocal(y0[:, 0, 0:STREAMED], sd[:, 0, 0:STREAMED]).then_inc(p_y0, 1)

            for i in range(NB):
                dve.wait_ge(sq_common, i + 1)
                nc.vector.scalar_tensor_tensor(out=a_m[:, i, :], in0=a_m[:, i, :], scalar=1.0, in1=a_m[:, i, :],
                                               op0=ALU.is_gt, op1=ALU.mult).then_inc(more_than_one, 1)
                dve.wait_ge(more_than_one, i + 1)
                nc.vector.tensor_tensor(a_m[:, i, :], a_m[:, i, :], adj_m[:, i, :], ALU.mult).then_inc(a_made, 1)

            dve.wait_ge(deg_done, 1)
            nc.vector.tensor_copy(col_v[:, :], deg_ps).then_inc(degv_made, 1)
            dve.wait_ge(degs_made, 1)
            link(nc.vector.tensor_scalar(col_y[:, :], col_s[:, :], TINY, None, ALU.max))
            link(nc.vector.reciprocal(dinv[:, :], col_y[:, :]))
            dve.wait_ge(degv_made, 1)
            refine(col_v[:, :], dinv[:, :])
            nc.vector.scalar_tensor_tensor(out=dinv[:, :], in0=col_v[:, :], scalar=0.0, in1=dinv[:, :],
                                           op0=ALU.is_gt, op1=ALU.mult).then_inc(dinv_made, 1)

            def lo_streamed(n, k):
                dve.wait_ge(p_hi, n + 1)
                nc.vector.tensor_tensor(xw_u[:, k, 1, :], xwp[1], xw_u[:, k, 0, :], ALU.subtract).then_inc(p_lo, 1)

            lo_streamed(0, 0)

            dve.wait_ge(s_done, 1)
            dve.wait_ge(dinv_made, 1)
            link(nc.vector.tensor_scalar(s_col[:, :], s_ps, 1e-20, None, ALU.max))
            link(nc.vector.reciprocal(c_col[:, :], s_col[:, :]))
            link(nc.vector.tensor_scalar(c_col[:, :], c_col[:, :], B_TOP, None, ALU.mult))
            nc.vector.scalar_tensor_tensor(out=r_col[:, :], in0=s_col[:, :], scalar=1.0 / B_TOP, in1=dinv[:, :],
                                           op0=ALU.mult, op1=ALU.mult).then_inc(rcol_made, 1)
            for j in range(NB):
                last = nc.vector.tensor_scalar(diag_c[:, j * P:(j + 1) * P], ident[:, :], c_col[:, j:j + 1], None,
                                               ALU.mult)
            last.then_inc(diagc_made, 1)

            dve.wait_ge(crow_made, 1)

            def scale_block(i):
                nc.vector.scalar_tensor_tensor(out=a_m[:, i, :], in0=a_m[:, i, :], scalar=dinv[:, i:i + 1], in1=c_row,
                                               op0=ALU.mult, op1=ALU.mult).then_inc(b_made, 1)

            scale_block(0)
            for i in range(1, NB, 2):
                scale_block(i)
                if i + 1 < NB:
                    scale_block(i + 1)
                dve.wait_ge(bhi_made, i + 1)
                nc.vector.tensor_tensor(b_lo[:, i, :], a_m[:, i, :], b_hi[:, i, :],
                                        ALU.subtract).then_inc(blo_dve, 1)
            lo_streamed(1, 1)
            dve.wait_ge(bias_loaded, 16)
            dve.wait_ge(rrow_made, 1)

            def finish(it, s, first):
                g, k = it * 2 + s // 4, s % 4
                dve.wait_ge(main_done, g * 4 + (k + 1))
                if not (first and s < 4):
                    dve.wait_ge(out_stored[k], g * 16)
                nc.vector.scalar_tensor_tensor(out=gout[:, k, :], in0=big[k % 2], scalar=w_back[:, 0:1],
                                               in1=rs_row[:, :], op0=ALU.mult, op1=ALU.mult).then_inc(scaled, 1)
                dve.wait_ge(x_loaded[s], it * 16 + (LOADS1 + 16))
                dve.wait_ge(scaled, g * 4 + (k + 1))
                nc.vector.scalar_tensor_tensor(out=gout[:, k, :], in0=gout[:, k, :], scalar=bias_c[:, 0:1],
                                               in1=x1[s], op0=ALU.add, op1=ALU.add).then_inc(out_made, 1)

            def pass2(it, first, last):
                for u in range(2):
                    g = it * 2 + u
                    more = not (last and u == 1)
                    if more:
                        nth = it if u == 0 else it + 1
                        for k in range(STREAMED):
                            streamed_moments((u + 1) % 2, nth, k, p_stats)
                        variance(0, STREAMED, p_stats, g * 3 + 6, p_mv, g + 2, p_ve)
                        dve.wait_ge(p_sd, g + 2)
                        nc.vector.reciprocal(y0[:, 0, 0:STREAMED], sd[:, 0, 0:STREAMED]).then_inc(p_y0, 1)
                    for k in range(4):
                        finish(it, 4 * u + k, first)
                        if first and u == 0 and k == 0:
                            lo_streamed(2, 2)
                        if more and k >= 1:
                            lo_streamed(g * 3 + (k + 2), k - 1)

            pass2(0, True, False)
            with dve.Fori(1, GROUPS // 2 - 1) as it:
                pass2(it, False, False)
            pass2(GROUPS // 2 - 1, False, True)

        @block.tensor
        def _(pe):
            pe.wait_ge(consts, 2)
            pe.wait_ge(w_loaded, 16)
            nc.tensor.transpose(wt_ps, w_in, ident[:, :]).then_inc(w_turned, 1)
            pe.wait_ge(w_scaled, 1)
            nc.tensor.transpose(ws_ps, w_t, ident[:, :]).then_inc(w_back_turned, 1)
            pe.wait_ge(w_ready, 1)

            def make_xw(dst, h_tile, signal):
                for j in range(NB):
                    mm = nc.tensor.matmul(dst[:, j * P:(j + 1) * P], h_tile[:, j * P:(j + 1) * P], w_s[:, :],
                                          start=True, stop=True)
                mm.then_inc(signal, 1)

            def pass1(it, first, last):
                for u in range(4):
                    g = it * 4 + u
                    for k in (2, 3):
                        h_tile = h1[(4 * u + k) % 8]
                        pe.wait_ge(h_made, g * 4 + (k + 1))
                        if k == 3:
                            if not (first and u < 2):
                                pe.wait_ge(lo_made, g - 1)
                            make_xw(xwp[u % 2], h_tile, xw_done)
                        for c in range(0, N, HALF):
                            mm = nc.tensor.matmul(sum_ps[:, c:c + HALF], ident[:, :], h_tile[:, c:c + HALF],
                                                  start=(first and u == 0 and k == 2),
                                                  stop=(last and u == 3 and k == 3), skip_group_check=True)
                        mm.then_inc(h_used, 1)

            pass1(0, True, False)
            with pe.Fori(1, GROUPS // 4 - 1) as it:
                pass1(it, False, False)
            pass1(GROUPS // 4 - 1, False, True)

            def spread(dst, diag, ready, signal):
                pe.wait_ge(ready, 1)
                for j in range(NB):
                    mm = nc.tensor.matmul(dst[:, j * P:(j + 1) * P], ones[:, :], diag[:, j * P:(j + 1) * P],
                                          start=True, stop=True)
                mm.then_inc(signal, 1)

            pe.wait_ge(lo_made, GROUPS)
            pe.wait_ge(sq_made, 1)
            for j in range(NB):
                mm = nc.tensor.matmul(norm_ps[:, j:j + 1], x_sq[:, j * P:(j + 1) * P], ones[:, 0:1],
                                      start=True, stop=True)
            mm.then_inc(norm_done, 1)
            spread(xwp[1], diag_c, diagn_made, rnrow_done)

            pe.wait_ge(xnrm_made, 1)
            for i in range(NB):
                if i >= 2:
                    pe.wait_ge(simh_made, i - 1)
                for c in range(0, N, HALF):
                    mm = nc.tensor.matmul(big[i % 2][:, c:c + HALF], x_nrm[:, i * P:(i + 1) * P],
                                          x_nrm[:, c:c + HALF], start=True, stop=True)
                mm.then_inc(sim_done, 1)

            pe.wait_ge(adj_made, NB)
            pe.wait_ge(simh_made, NB)
            for i in range(NB):
                if i >= 2:
                    pe.wait_ge(nm_odd if i % 2 else nm_even, i // 2)
                dst = big[i % 2]
                for c in range(0, N, HALF):
                    nc.tensor.matmul(dst[:, c:c + HALF], ident16[:, :], adj_m[:, i, c:c + HALF],
                                     start=True, stop=False, skip_group_check=True)
                for j in range(NB):
                    nc.tensor.matmul(dst[:, j * P:(j + 1) * P], adj_m[:, j, i * P:(i + 1) * P], ident16[:, :],
                                     start=False, stop=False, skip_group_check=True)
                nc.tensor.matmul(dst[:, i * P:(i + 1) * P], ident16[:, :], ident16[:, :],
                                 start=False, stop=True, skip_group_check=True).then_inc(sym_done, 1)

            def degree(i):
                pe.wait_ge(a_made, i + 1)
                for j in range(NB):
                    mm = nc.tensor.matmul(deg_ps[:, j:j + 1], a_m[:, i, j * P:(j + 1) * P], ones[:, 0:1],
                                          start=(i == 0 and j == 0), stop=(i == NB - 1), skip_group_check=True)
                return mm

            pe.wait_ge(nm_even, NB // 2)
            pe.wait_ge(nm_odd, NB // 2)
            for i in range(NB):
                if i >= 2:
                    pe.wait_ge(sq_common, i - 1)
                for kb in range(NB):
                    for c in range(0, N, HALF):
                        mm = nc.tensor.matmul(big[i % 2][:, c:c + HALF], nm_m[:, kb, i * P:(i + 1) * P],
                                              nm_m[:, kb, c:c + HALF], start=(kb == 0), stop=(kb == NB - 1))
                mm.then_inc(common_done, 1)
                if i >= 2:
                    degree(i - 2)

            def xw_streamed(n, k):
                pe.wait_ge(p_h, n + 1)
                if not isinstance(n, int) or n >= 1:
                    pe.wait_ge(p_lo, n)
                make_xw(xwp[1], h1[k], p_xw)

            xw_streamed(0, 0)
            degree(NB - 2)
            degree(NB - 1).then_inc(deg_done, 1)

            pe.wait_ge(dinv_made, 1)
            for i in range(NB):
                for j in range(NB):
                    mm = nc.tensor.matmul(s_ps[:, j:j + 1], a_m[:, i, j * P:(j + 1) * P], dinv[:, i:i + 1],
                                          start=(i == 0 and j == 0), stop=(i == NB - 1), skip_group_check=True)
            mm.then_inc(s_done, 1)
            xw_streamed(1, 1)
            pe.wait_ge(sq_common, NB)
            spread(big[0], diag_c, diagc_made, crow_done)
            spread(big[1], diag_r, diagr_made, rrow_done)

            def node_product(g, k, hi, lo, first):
                dst = big[k % 2]
                for j in range(NB):
                    if first:
                        pe.wait_ge(bhi_made, j + 1)
                        pe.wait_ge(blo_dve if j % 2 else blo_pool, j // 2 + 1)
                    for xw, parts in ((hi, (b_hi, b_lo)), (lo, (b_hi,))):
                        for part in parts:
                            for c in range(0, N, HALF):
                                mm = nc.tensor.matmul(dst[:, c:c + HALF], xw[:, j * P:(j + 1) * P],
                                                      part[:, j, c:c + HALF],
                                                      start=(j == 0 and xw is hi and part is b_hi),
                                                      stop=(j == NB - 1 and xw is lo))
                mm.then_inc(main_done, 1)

            def pass2(it, first, last):
                for u in range(2):
                    g = it * 2 + u
                    for k in range(4):
                        opening = first and u == 0
                        if opening and k < 2:
                            pe.wait_ge(rrow_made if k else crow_made, 1)
                        else:
                            pe.wait_ge(scaled, g * 4 + (k - 1))
                        if k < STREAMED:
                            pe.wait_ge(p_lo, g * 3 + (k + 1))
                            node_product(g, k, xw_u[:, k, 0, :], xw_u[:, k, 1, :], opening and k == 0)
                        else:
                            node_product(g, k, cached_xw(g, 0), cached_xw(g, 1), False)
                        if opening and k == 0:
                            xw_streamed(2, 2)
                        if k >= 1 and not (last and u == 1):
                            xw_streamed(g * 3 + (k + 2), k - 1)

            pass2(0, True, False)
            with pe.Fori(1, GROUPS // 2 - 1) as it:
                pass2(it, False, False)
            pass2(GROUPS // 2 - 1, False, True)


_INS = ['x', 'adj', 'L0_gnn_bias', 'L0_gnn_gumbel']
_OUTS = [((64, 128, 1024), 'float32')]


def kernel(**inputs):
    import numpy as _np
    import concourse.bacc as _bacc
    from concourse import mybir as _mybir
    from concourse.bass_utils import run_bass_kernel_spmd as _run

    nc = _bacc.Bacc("TRN2", target_bir_lowering=False, num_devices=1)
    arrays, args = {}, []
    for name in _INS:
        a = _np.ascontiguousarray(inputs[name])
        arrays[f"in_{name}_dram"] = a
        args.append(nc.dram_tensor(f"in_{name}_dram", a.shape, _mybir.dt.from_np(a.dtype), kind="ExternalInput").ap())
    for i, (shape, dtype) in enumerate(_OUTS):
        dt = _mybir.dt.from_np(_np.dtype(dtype))
        args.append(nc.dram_tensor(f"out_{i}_dram", shape, dt, kind="ExternalOutput").ap())
    bass_preln_graph_layer(nc, *args)
    r = _run(nc, [arrays], core_ids=[0])
    got = tuple(r.results[0][f"out_{i}_dram"] for i in range(len(_OUTS)))
    return got[0]
```

```python
from contextlib import ExitStack

import concourse.bass as bass
from concourse import mybir


def bass_preln_graph_layer(
    nc: bass.Bass,
    x: bass.AP,
    adj: bass.AP,
    bias: bass.AP,
    gumbel: bass.AP,
    out: bass.AP,
):
    fp32 = mybir.dt.float32
    fp16 = mybir.dt.float16
    int32 = mybir.dt.int32
    ALU = mybir.AluOpType
    ACT = mybir.ActivationFunctionType
    AX = mybir.AxisListType

    B, T, N = x.shape
    P = 128
    NB = N // P
    HALF = 512
    GROUPS = B // 4
    STREAMED = 3
    G_RING = 6
    LN_EPS = 1e-5
    NORM_EPS = 1e-12
    W_TOP = 2.0 ** 9
    H_UP = 2.0 ** 10
    B_UP = 2.0 ** 12
    C_DOWN = 1.0 / 8
    A_ONE = C_DOWN ** 2
    TINY = 1e-18
    EXPONENT = 0x7F800000

    def entry(g, k):
        return g if k == STREAMED else GROUPS + STREAMED * g + k

    gumbel_block = gumbel.rearrange("(i p j) c -> i p (j c)", p=P, j=N)

    ctx = ExitStack()
    with ctx:
        def sb(name, shape, dt=fp32):
            return ctx.enter_context(nc.sbuf_tensor(name, shape, dt))

        def sem(name):
            return ctx.enter_context(nc.semaphore(name))

        cache = sb("cache", [P, GROUPS * 2 * N], fp16)
        xw_u = sb("xw_u", [P, STREAMED, 2, N], fp16)
        xring = sb("xring", [P, 8, N])
        region_a = sb("region_a", [P, 8, N])
        hring = sb("hring", [P, STREAMED, N])
        adj_m = sb("adj_m", [P, NB, N], fp16)
        nm_m = sb("nm_m", [P, NB, N], fp16)
        gout = sb("gout", [P, 4, N])
        rs_row = sb("rs_row", [P, N])

        adj_f = adj_m[:, :, :].rearrange("p a n -> p (a n)").bitcast(fp32)
        nm_f = nm_m[:, :, :].rearrange("p a n -> p (a n)").bitcast(fp32)
        b_hi, b_lo = nm_m, adj_m
        a_m = region_a

        x1 = [xring[:, s, :] for s in range(8)] + [region_a[:, s, :] for s in range(8)]
        h1 = [hring[:, s, :] for s in range(3)] + [adj_f[:, s * N:(s + 1) * N] for s in range(4)] + [nm_f[:, 0:N]]
        pool_sum = nm_f[:, N:2 * N]
        xring_f = xring[:, :, :].rearrange("p a n -> p (a n)")
        goutf = gout[:, :, :].rearrange("p a n -> p (a n)")
        gum = [goutf[:, 0:2 * N], goutf[:, 2 * N:4 * N], nm_f[:, 2 * N:4 * N], xring_f[:, 0:2 * N],
               xring_f[:, 2 * N:4 * N], nm_f[:, 0:2 * N]]
        sim_h = [region_a[:, s, :] for s in (0, 1)]
        one_m = [region_a[:, s, :] for s in (2, 3)]
        score0 = [region_a[:, s, :] for s in (4, 5)]
        score1 = [region_a[:, s, :] for s in (6, 7)]
        x_sum = xring[:, 4, :]
        x_nrm = xring[:, 5, :]
        x_sq = xring[:, 6, :]
        diag_n = xring[:, 7, :]
        xw_uf = xw_u[:, :, :, :].rearrange("p k a n -> p (k a n)").bitcast(fp32)
        a_hi = adj_m
        a_lo = goutf.bitcast(fp16).rearrange("p (a n) -> p a n", n=N)
        h32_first = [xw_uf[:, N:2 * N], xw_uf[:, 2 * N:3 * N], rs_row[:, :]]
        h32_later = [region_a[:, k, :] for k in range(STREAMED)]
        h16 = [hring[:, k, :].bitcast(fp16).rearrange("p (a n) -> p a n", n=N) for k in range(STREAMED)]
        c_row = gout[:, 0, :]
        diag_d = gout[:, 1, :]
        s_row = gout[:, 2, :]
        pow_row = gout[:, 2, :]
        dinv_b = gout[:, 3, 0:HALF].bitcast(fp16).rearrange("p (a n) -> p a n", n=P)

        w_in = gout[:, 3, 0:P]
        w_t = gout[:, 3, P:2 * P]
        w_s = sb("w_s", [P, P])
        w16 = sb("w16", [P, 2, P], fp16)
        ones16 = sb("ones16", [P, 2], fp16)
        ident = sb("ident", [P, P])
        ident16 = sb("ident16", [P, P], fp16)
        ones = sb("ones", [P, P])
        bias_c = sb("bias_c", [P, 1])
        l1 = sb("l1", [P, 1])
        w_pow = sb("w_pow", [P, 1])
        w_up = sb("w_up", [P, 1])
        w_back = sb("w_back", [P, 1])
        stats = sb("stats", [P, 2, 4, 2, 6])
        mv = sb("mv", [P, 2, 4, 2])
        ve4 = sb("ve4", [P, 2, 4])
        sd = sb("sd", [P, 2, 4])
        y0 = sb("y0", [P, 2, 4])
        nt = sb("nt", [P, 2, 4])
        rstd = sb("rstd", [P, 2, 4])
        nmr = sb("nmr", [P, 2, 4])
        threes = sb("threes", [P, 4])
        zeros = sb("zeros", [P, 4])
        wait_pad = sb("wait_pad", [P, 1])
        col_v = sb("col_v", [P, NB])
        col_s = sb("col_s", [P, NB])
        col_y = sb("col_y", [P, NB])
        col_t = sb("col_t", [P, NB])
        rnorm = sb("rnorm", [P, NB])
        dinv = sb("dinv", [P, NB])
        dinv_up = sb("dinv_up", [P, NB])

        psum = ctx.enter_context(nc.psum_tensor("psum", [P, 8 * HALF], fp32))
        big = [psum[:, 0:N], psum[:, N:2 * N]]
        xwp = [psum[:, 2 * N:3 * N], psum[:, 3 * N:4 * N]]
        sum_ps = big[0]
        wt_ps = big[1][:, 0:P]
        ws_ps = big[1][:, HALF:HALF + P]
        norm_ps = big[1][:, 0:NB]
        deg_ps = xwp[0][:, 0:NB]
        sym_ps = big + xwp

        consts = sem("consts")
        w_loaded = sem("w_loaded")
        bias_loaded = sem("bias_loaded")
        w_turned = sem("w_turned")
        w_scaled = sem("w_scaled")
        w_back_turned = sem("w_back_turned")
        w_ready = sem("w_ready")
        x_loaded = [sem(f"x_loaded{s}") for s in range(16)]
        g_loaded = [sem(f"g_loaded{s}") for s in range(G_RING)]
        dve_step = sem("dve_step")
        pool_step = sem("pool_step")
        stats_made = sem("stats_made")
        mv_made = sem("mv_made")
        ve_made = sem("ve_made")
        sd_made = sem("sd_made")
        y0_made = sem("y0_made")
        rstd_made = sem("rstd_made")
        h_made = sem("h_made")
        h_used = sem("h_used")
        pool_added = sem("pool_added")
        xw_done = sem("xw_done")
        hi_made = sem("hi_made")
        lo_made = sem("lo_made")
        xsum_made = sem("xsum_made")
        sq_made = sem("sq_made")
        norm_done = sem("norm_done")
        normv_made = sem("normv_made")
        norms_made = sem("norms_made")
        diagn_made = sem("diagn_made")
        rnrow_done = sem("rnrow_done")
        xnrm_made = sem("xnrm_made")
        sim_done = sem("sim_done")
        simh_made = sem("simh_made")
        onem_made = sem("onem_made")
        score0_made = sem("score0_made")
        score1_made = sem("score1_made")
        adj_made = sem("adj_made")
        sym_done = sem("sym_done")
        nm_even = sem("nm_even")
        nm_odd = sem("nm_odd")
        common_done = sem("common_done")
        sq_common = sem("sq_common")
        more_than_one = sem("more_than_one")
        a_made = sem("a_made")
        deg_done = sem("deg_done")
        degv_made = sem("degv_made")
        degs_made = sem("degs_made")
        dinv_made = sem("dinv_made")
        s_done = sem("s_done")
        ahi_made = sem("ahi_made")
        alo_pool = sem("alo_pool")
        alo_dve = sem("alo_dve")
        dinvb_made = sem("dinvb_made")
        diagd_made = sem("diagd_made")
        drow_done = sem("drow_done")
        srow_made = sem("srow_made")
        crow_made = sem("crow_made")
        rrow_made = sem("rrow_made")
        b_made = sem("b_made")
        bhi_made = sem("bhi_made")
        blo_dve = sem("blo_dve")
        blo_pool = sem("blo_pool")
        p_stats = sem("p_stats")
        p_mv = sem("p_mv")
        p_ve = sem("p_ve")
        p_sd = sem("p_sd")
        p_y0 = sem("p_y0")
        p_rstd = sem("p_rstd")
        p_h = sem("p_h")
        p_hlo = sem("p_hlo")
        p_xw = sem("p_xw")
        p_hi = sem("p_hi")
        p_lo = sem("p_lo")
        main_done = sem("main_done")
        scaled = sem("scaled")
        out_made = sem("out_made")
        out_stored = [sem(f"out_stored{s}") for s in range(4)]

        block = ctx.enter_context(nc.Block())

        def cached_xw(g, part):
            at = (g * 2 + part) * N
            return cache[:, bass.ds(at, N)]

        @block.sync
        def _(sp):
            def load_x(slot, g, k):
                sp.dma_start(x1[slot], x[entry(g, k), :, :]).then_inc(x_loaded[slot], 16)

            def load_gumbel(i):
                sp.dma_start(gum[i % G_RING], gumbel_block[i, :, :]).then_inc(g_loaded[i % G_RING], 16)

            load_x(0, 0, 0)
            load_x(1, 0, 1)
            sp.dma_start(w_in, adj).then_inc(w_loaded, 16)
            for s in range(2, 16):
                load_x(s, s // 4, s % 4)
            sp.dma_start(bias_c[:, :], bias.rearrange("(p a) -> p a", a=1)).then_inc(bias_loaded, 16)
            with sp.Fori(1, GROUPS // 4) as it:
                for s in range(16):
                    sp.wait_ge(h_made, it * 16 + (s - 15))
                    load_x(s, it * 4 + s // 4, s % 4)

            for i in range(3):
                load_gumbel(i)
            for i, slots in ((3, (0, 1)), (4, (2, 3))):
                for s in slots:
                    sp.wait_ge(h_made, 4 * GROUPS - 15 + s)
                load_gumbel(i)
            sp.wait_ge(xsum_made, 1)
            sp.wait_ge(xw_done, GROUPS)
            load_gumbel(5)
            for i in range(G_RING, NB):
                sp.wait_ge(adj_made, i - G_RING + 1)
                load_gumbel(i)
            for s in range(4):
                if s % 2 == 0:
                    sp.wait_ge(adj_made, 4 + s // 2)
                load_x(s, 0, s)
            sp.wait_ge(sim_done, NB)
            for s in range(4, 8):
                load_x(s, 1, s - 4)

            def store(g, k):
                sp.wait_ge(out_made, 4 * g + (k + 1))
                sp.dma_start(out[entry(g, k), :, :], gout[:, k, :]).then_inc(out_stored[k], 16)

            with sp.Fori(0, GROUPS // 2 - 1) as it:
                for s in range(8):
                    store(it * 2 + s // 4, s % 4)
                    load_x(s, it * 2 + (s // 4 + 2), s % 4)
            for s in range(8):
                store(GROUPS - 2 + s // 4, s % 4)
            for k in range(4):
                sp.wait_ge(out_stored[k], 16 * GROUPS)

        @block.gpsimd
        def _(pool):
            step = [0]

            def link(ins):
                step[0] += 1
                ins.then_inc(pool_step, 1)
                pool.wait_ge(pool_step, step[0])

            link(nc.gpsimd.memset(ident[:, :], 0.0))
            link(nc.gpsimd.affine_select(out=ident[:, :], in_=ident[:, :], compare_op=ALU.not_equal, fill=1.0,
                                         base=0, pattern=[[-1, P]], channel_multiplier=1))
            nc.gpsimd.tensor_copy(ident16[:, :], ident[:, :]).then_inc(consts, 1)
            link(nc.gpsimd.memset(ones16[:, :], 1.0))
            nc.gpsimd.memset(ones[:, :], 1.0).then_inc(consts, 1)
            link(nc.gpsimd.memset(threes[:, :], 3.0))
            link(nc.gpsimd.memset(zeros[:, :], 0.0))
            nc.gpsimd.memset(pool_sum, 0.0).then_inc(pool_added, 1)

            def newton(q, kk, y_ready, count, signal, base):
                pool.wait_ge(y_ready, count)
                y, v, t, r, m = y0[:, q, 0:kk], ve4[:, q, 0:kk], nt[:, q, 0:kk], rstd[:, q, 0:kk], nmr[:, q, 0:kk]
                nc.gpsimd.tensor_tensor(t, y, y, ALU.mult).then_inc(pool_step, 1)
                pool.wait_ge(pool_step, base + 1)
                nc.gpsimd.tensor_tensor(t, t, v, ALU.mult).then_inc(pool_step, 1)
                pool.wait_ge(pool_step, base + 2)
                nc.gpsimd.tensor_tensor(t, threes[:, 0:kk], t, ALU.subtract).then_inc(pool_step, 1)
                pool.wait_ge(pool_step, base + 3)
                nc.gpsimd.tensor_tensor(r, y, t, ALU.mult).then_inc(pool_step, 1)
                pool.wait_ge(pool_step, base + 4)
                nc.gpsimd.tensor_tensor(m, mv[:, q, 0:kk, 0], r, ALU.mult).then_inc(pool_step, 1)
                pool.wait_ge(pool_step, base + 5)
                nc.gpsimd.tensor_tensor(m, zeros[:, 0:kk], m, ALU.subtract).then_inc(signal, 1)

            base1 = step[0]
            def add(it, u, k):
                pool.wait_ge(h_made, it * 16 + (4 * u + k + 1))
                pool.wait_ge(pool_added, it * 8 + (2 * u + k + 1))
                nc.gpsimd.tensor_tensor(pool_sum, pool_sum, h1[(4 * u + k) % 8], ALU.add).then_inc(pool_added, 1)

            def pass1(it, first):
                for u in range(4):
                    newton(u % 2, 4, y0_made, it * 4 + (u + 1), rstd_made, it * 20 + (base1 + 5 * u))
                    if not (first and u == 0):
                        add(*((it, u - 1) if u else (it - 1, 3)), 1)
                    add(it, u, 0)

            pass1(0, True)
            with pool.Fori(1, GROUPS // 4) as it:
                pass1(it, False)
            add(GROUPS // 4 - 1, 3, 1)

            for i in range(NB):
                pool.wait_ge(onem_made, i + 1)
                pool.wait_ge(g_loaded[i % G_RING], 16 * (i // G_RING + 1))
                if i >= 2:
                    pool.wait_ge(adj_made, i - 1)
                nc.gpsimd.tensor_tensor(score1[i % 2], one_m[i % 2], gum[i % G_RING][:, 1:2 * N:2],
                                        ALU.add).then_inc(score1_made, 1)

            base2 = base1 + 5 * GROUPS
            newton(0, STREAMED, p_y0, 1, p_rstd, base2)
            for i in range(NB - 1):
                pool.wait_ge(ahi_made, i + 1)
                nc.gpsimd.tensor_tensor(a_lo[:, i, :], a_m[:, i, :], a_hi[:, i, :],
                                        ALU.subtract).then_inc(alo_pool, 1)
            pool.wait_ge(deg_done, 1)
            pool.wait_ge(dinv_made, 1)
            for j in range(NB):
                last = nc.gpsimd.tensor_tensor(diag_d[:, j * P:(j + 1) * P], ident[:, :],
                                               dinv[:, j:j + 1].to_broadcast([P, P]), ALU.mult)
            last.then_inc(diagd_made, 1)
            for i in range(0, NB, 2):
                pool.wait_ge(bhi_made, i + 1)
                nc.gpsimd.tensor_tensor(b_lo[:, i, :], a_m[:, i, :], b_hi[:, i, :],
                                        ALU.subtract).then_inc(blo_pool, 1)

            with pool.Fori(1, GROUPS) as g:
                newton(0, STREAMED, p_y0, g + 1, p_rstd, g * 5 + base2)

        @block.scalar
        def _(act):
            def normalise(x_tile, h_tile, q, k, signal):
                ins = nc.scalar.activation(h_tile, x_tile, ACT.Relu, bias=nmr[:, q, k:k + 1],
                                           scale=rstd[:, q, k:k + 1])
                if signal is not None:
                    ins.then_inc(signal, 1)

            def root(q, kk, signal):
                nc.scalar.activation(sd[:, q, 0:kk], ve4[:, q, 0:kk], ACT.Sqrt).then_inc(signal, 1)

            def hi_cached(g, u):
                act.wait_ge(xw_done, g + 1)
                nc.scalar.activation(cached_xw(g, 0), xwp[u], ACT.Copy).then_inc(hi_made, 1)

            act.wait_ge(ve_made, 1)
            root(0, 4, sd_made)

            def pass1(it, first, last):
                for u in range(4):
                    g = it * 4 + u
                    act.wait_ge(rstd_made, g + 1)
                    for k in range(4):
                        if not (first and u < 2):
                            if k < 2:
                                act.wait_ge(pool_added, g * 2 + (k - 2))
                            else:
                                act.wait_ge(h_used if k == 2 else xw_done, g * 2 - 3 if k == 2 else g - 1)
                        normalise(x1[4 * u + k], h1[(4 * u + k) % 8], u % 2, k, h_made)
                    if not (last and u == 3):
                        act.wait_ge(ve_made, g + 2)
                        root((u + 1) % 2, 4, sd_made)
                    if not (first and u == 0):
                        hi_cached(g - 1, (u + 1) % 2)

            pass1(0, True, False)
            with act.Fori(1, GROUPS // 4 - 1) as it:
                pass1(it, False, False)
            pass1(GROUPS // 4 - 1, False, True)

            act.wait_ge(xsum_made, 1)
            nc.scalar.activation(x_sq, x_sum, ACT.Square).then_inc(sq_made, 1)
            hi_cached(GROUPS - 1, 1)
            act.wait_ge(normv_made, 1)
            nc.scalar.activation(col_s[:, :], col_v[:, :], ACT.Sqrt).then_inc(norms_made, 1)

            for i in range(NB):
                act.wait_ge(sim_done, i + 1)
                if i >= 2:
                    act.wait_ge(score0_made, i - 1)
                nc.scalar.activation(sim_h[i % 2], big[i % 2], ACT.Copy, scale=0.5, bias=0.5).then_inc(simh_made, 1)
                act.wait_ge(simh_made, i + 1)
                if i >= 2:
                    act.wait_ge(score1_made, i - 1)
                nc.scalar.activation(one_m[i % 2], sim_h[i % 2], ACT.Copy, scale=-1.0, bias=1.0).then_inc(onem_made, 1)

            for i in range(0, NB, 2):
                act.wait_ge(sym_done, i + 1)
                nc.scalar.activation(nm_m[:, i, :], sym_ps[i % 4], ACT.Sign).then_inc(nm_even, 1)

            def normalise_streamed(x_tile, h32, k):
                normalise(x_tile, h32, 0, k, None)
                normalise(x_tile, h16[k][:, 0, :], 0, k, p_h)

            def high_a(i):
                act.wait_ge(a_made, i + 1)
                nc.scalar.activation(a_hi[:, i, :], a_m[:, i, :], ACT.Copy).then_inc(ahi_made, 1)

            for i in range(NB):
                act.wait_ge(common_done, i + 1)
                nc.scalar.activation(a_m[:, i, :], big[i % 2], ACT.Square, scale=C_DOWN).then_inc(sq_common, 1)
                if i == 0:
                    act.wait_ge(p_ve, 1)
                    root(0, STREAMED, p_sd)
                if i >= 1:
                    high_a(i - 1)
                    k = (i - 1) // 2
                    if i == 1:
                        act.wait_ge(p_rstd, 1)
                    if i % 2 == 1 and k < STREAMED:
                        normalise(x1[k], h32_first[k], 0, k, None)
                    elif k < STREAMED:
                        normalise(x1[k], h16[k][:, 0, :], 0, k, p_h)
            high_a(NB - 1)

            def hi_streamed(n, k, src=xwp[1]):
                act.wait_ge(p_xw, n + 1)
                nc.scalar.activation(xw_u[:, k, 0, :], src, ACT.Copy, scale=1.0 / H_UP).then_inc(p_hi, 1)

            hi_streamed(0, 0)
            act.wait_ge(degv_made, 1)
            nc.scalar.activation(col_s[:, :], col_v[:, :], ACT.Sqrt).then_inc(degs_made, 1)
            act.wait_ge(s_done, 1)
            nc.scalar.activation(s_row, big[0], ACT.Copy, bias=1e-20).then_inc(srow_made, 1)
            for i in range(NB):
                act.wait_ge(b_made, i + 1)
                nc.scalar.activation(b_hi[:, i, :], a_m[:, i, :], ACT.Copy).then_inc(bhi_made, 1)
            hi_streamed(1, 1, xwp[0])
            hi_streamed(2, 2)

            def pass2(it, us):
                for u in us:
                    g = it * 2 + u
                    act.wait_ge(p_ve, g + 2)
                    root(0, STREAMED, p_sd)
                    act.wait_ge(p_rstd, g + 2)
                    for k in range(STREAMED):
                        act.wait_ge(p_xw, g * 3 + (k + 1))
                        normalise_streamed(x1[4 * ((u + 1) % 2) + k], h32_later[k], k)
                    for k in range(STREAMED):
                        act.wait_ge(main_done, g * 4 + (k + 1))
                        hi_streamed(g * 3 + (k + 3), k)

            with act.Fori(0, GROUPS // 2 - 1) as it:
                pass2(it, (0, 1))
            pass2(GROUPS // 2 - 1, (0,))

        @block.vector
        def _(dve):
            step = [0]

            def link(ins):
                step[0] += 1
                ins.then_inc(dve_step, 1)
                dve.wait_ge(dve_step, step[0])

            def moments(x_tile, q, k, signal):
                nc.vector.bn_stats(stats[:, q, k, 0, :], x_tile[:, 0:HALF])
                nc.vector.bn_stats(stats[:, q, k, 1, :], x_tile[:, HALF:N]).then_inc(signal, 1)

            def variance(q, kk, up, stats_sem, n_stats, mv_sem, n_mv, ve_sem):
                dve.wait_ge(stats_sem, n_stats)
                nc.vector.memset(wait_pad[:, :], 0.0)
                for k in range(kk):
                    last = nc.vector.bn_aggr(mv[:, q, k, :], stats[:, q, k, :, :])
                last.then_inc(mv_sem, 1)
                dve.wait_ge(mv_sem, n_mv)
                nc.vector.tensor_scalar(ve4[:, q, 0:kk], mv[:, q, 0:kk, 1], LN_EPS, 4.0 / up ** 2, ALU.add,
                                        ALU.mult).then_inc(ve_sem, 1)

            def lo_cached(g, u):
                dve.wait_ge(hi_made, g + 1)
                nc.vector.tensor_tensor(cached_xw(g, 1), xwp[u], cached_xw(g, 0), ALU.subtract).then_inc(lo_made, 1)

            def tile_moments(it, u, k):
                dve.wait_ge(x_loaded[4 * u + k], it * 16 + 16)
                moments(x1[4 * u + k], u % 2, k, stats_made)

            for k in range(4):
                tile_moments(0, 0, k)
            variance(0, 4, 1.0, stats_made, 4, mv_made, 1, ve_made)

            dve.wait_ge(w_turned, 1)
            link(nc.vector.tensor_reduce(l1[:, :], wt_ps, AX.X, ALU.add, apply_absolute_value=True))
            link(nc.vector.tensor_scalar(l1[:, :], l1[:, :], 1e-30, None, ALU.max))
            link(nc.vector.tensor_scalar(w_pow[:, :].bitcast(int32), l1[:, :].bitcast(int32), EXPONENT, None,
                                         ALU.bitwise_and))
            link(nc.vector.reciprocal(w_up[:, :], w_pow[:, :]))
            link(nc.vector.tensor_scalar(w_up[:, :], w_up[:, :], W_TOP, None, ALU.mult))
            link(nc.vector.tensor_scalar(w_back[:, :], w_pow[:, :], 1.0 / W_TOP, None, ALU.mult))
            nc.vector.tensor_scalar(w_t, wt_ps, w_up[:, 0:1], None, ALU.mult).then_inc(w_scaled, 1)
            dve.wait_ge(w_back_turned, 1)
            link(nc.vector.tensor_copy(w_s[:, :], ws_ps))
            link(nc.vector.tensor_copy(w16[:, 0, :], w_s[:, :]))
            nc.vector.tensor_tensor(w16[:, 1, :], w_s[:, :], w16[:, 0, :], ALU.subtract).then_inc(w_ready, 1)

            def pass1(it, first, last):
                for u in range(4):
                    g = it * 4 + u
                    more = not (last and u == 3)
                    nxt = (it, u + 1) if u < 3 else (it + 1, 0)
                    if more:
                        tile_moments(*nxt, 0)
                    dve.wait_ge(sd_made, g + 1)
                    nc.vector.reciprocal(y0[:, u % 2, :], sd[:, u % 2, :]).then_inc(y0_made, 1)
                    if more:
                        for k in range(1, 4):
                            tile_moments(*nxt, k)
                    if not (first and u < 2):
                        lo_cached(g - 2, u % 2)
                    if more:
                        variance((u + 1) % 2, 4, 1.0, stats_made, g * 4 + 8, mv_made, g + 2, ve_made)

            pass1(0, True, False)
            with dve.Fori(1, GROUPS // 4 - 1) as it:
                pass1(it, False, False)
            pass1(GROUPS // 4 - 1, False, True)

            dve.wait_ge(h_used, 2 * GROUPS)
            dve.wait_ge(pool_added, 2 * GROUPS + 1)
            nc.vector.tensor_tensor(x_sum, sum_ps, pool_sum, ALU.add).then_inc(xsum_made, 1)

            def refine(v, y):
                link(nc.vector.tensor_tensor(col_t[:, :], y, y, ALU.mult))
                link(nc.vector.tensor_tensor(col_t[:, :], col_t[:, :], v, ALU.mult))
                link(nc.vector.tensor_scalar(col_t[:, :], col_t[:, :], -0.5, 1.5, ALU.mult, ALU.add))
                link(nc.vector.tensor_tensor(y, y, col_t[:, :], ALU.mult))

            dve.wait_ge(norm_done, 1)
            nc.vector.tensor_copy(col_v[:, :], norm_ps).then_inc(normv_made, 1)
            dve.wait_ge(norms_made, 1)
            link(nc.vector.tensor_scalar(col_y[:, :], col_s[:, :], TINY, None, ALU.max))
            link(nc.vector.reciprocal(rnorm[:, :], col_y[:, :]))
            dve.wait_ge(normv_made, 1)
            refine(col_v[:, :], rnorm[:, :])
            link(nc.vector.tensor_scalar(rnorm[:, :], rnorm[:, :], 1.0 / (B * NORM_EPS), None, ALU.min))
            for j in range(NB):
                last = nc.vector.tensor_scalar(diag_n[:, j * P:(j + 1) * P], ident[:, :], rnorm[:, j:j + 1], None,
                                               ALU.mult)
            last.then_inc(diagn_made, 1)
            lo_cached(GROUPS - 2, 0)
            lo_cached(GROUPS - 1, 1)
            dve.wait_ge(rnrow_done, 1)
            dve.wait_ge(xsum_made, 1)
            nc.vector.tensor_tensor(x_nrm, x_sum, big[1], ALU.mult).then_inc(xnrm_made, 1)

            def make_score0(i):
                dve.wait_ge(simh_made, i + 1)
                dve.wait_ge(g_loaded[i % G_RING], 16 * (i // G_RING + 1))
                if i >= 2:
                    dve.wait_ge(adj_made, i - 1)
                nc.vector.tensor_tensor(score0[i % 2], sim_h[i % 2], gum[i % G_RING][:, 0:2 * N:2],
                                        ALU.add).then_inc(score0_made, 1)

            make_score0(0)
            for i in range(NB):
                if i + 1 < NB:
                    make_score0(i + 1)
                dve.wait_ge(score1_made, i + 1)
                dve.wait_ge(score0_made, i + 1)
                nc.vector.tensor_tensor(adj_m[:, i, :], score0[i % 2], score1[i % 2], ALU.is_gt).then_inc(adj_made, 1)

            for i in range(1, NB, 2):
                dve.wait_ge(sym_done, i + 1)
                nc.vector.tensor_scalar(nm_m[:, i, :], sym_ps[i % 4], 1.0, None, ALU.min).then_inc(nm_odd, 1)

            LOADS1 = 16 * (GROUPS // 4)

            def streamed_moments(q, nth, k, signal):
                dve.wait_ge(x_loaded[4 * q + k], nth * 16 + (LOADS1 + 16))
                moments(x1[4 * q + k], 0, k, signal)

            for k in range(STREAMED):
                streamed_moments(0, 0, k, p_stats)
            variance(0, STREAMED, H_UP, p_stats, STREAMED, p_mv, 1, p_ve)

            def low_h(n, h32, k):
                dve.wait_ge(p_h, n + 1)
                nc.vector.tensor_tensor(h16[k][:, 1, :], h32, h16[k][:, 0, :], ALU.subtract).then_inc(p_hlo, 1)

            for i in range(NB):
                dve.wait_ge(sq_common, i + 1)
                nc.vector.scalar_tensor_tensor(out=a_m[:, i, :], in0=a_m[:, i, :], scalar=A_ONE, in1=a_m[:, i, :],
                                               op0=ALU.is_gt, op1=ALU.mult).then_inc(more_than_one, 1)
                dve.wait_ge(more_than_one, i + 1)
                nc.vector.tensor_tensor(a_m[:, i, :], a_m[:, i, :], adj_m[:, i, :], ALU.mult).then_inc(a_made, 1)
                if i == 0:
                    dve.wait_ge(p_sd, 1)
                    nc.vector.reciprocal(y0[:, 0, 0:STREAMED], sd[:, 0, 0:STREAMED]).then_inc(p_y0, 1)
                if i >= 2 and i % 2 == 0:
                    low_h(i // 2 - 1, h32_first[i // 2 - 1], i // 2 - 1)
            dve.wait_ge(ahi_made, NB)
            nc.vector.tensor_tensor(a_lo[:, NB - 1, :], a_m[:, NB - 1, :], a_hi[:, NB - 1, :],
                                    ALU.subtract).then_inc(alo_dve, 1)

            dve.wait_ge(deg_done, 1)
            nc.vector.tensor_copy(col_v[:, :], deg_ps).then_inc(degv_made, 1)
            dve.wait_ge(degs_made, 1)
            link(nc.vector.tensor_scalar(col_y[:, :], col_s[:, :], TINY, None, ALU.max))
            link(nc.vector.reciprocal(dinv[:, :], col_y[:, :]))
            dve.wait_ge(degv_made, 1)
            refine(col_v[:, :], dinv[:, :])
            nc.vector.scalar_tensor_tensor(out=dinv[:, :], in0=col_v[:, :], scalar=0.0, in1=dinv[:, :],
                                           op0=ALU.is_gt, op1=ALU.mult).then_inc(dinv_made, 1)

            def lo_streamed(n, k, src=xwp[1]):
                dve.wait_ge(p_hi, n + 1)
                nc.vector.scalar_tensor_tensor(out=xw_u[:, k, 1, :], in0=src, scalar=1.0 / H_UP,
                                               in1=xw_u[:, k, 0, :], op0=ALU.mult, op1=ALU.subtract).then_inc(p_lo, 1)

            dve.wait_ge(dinv_made, 1)
            dve.wait_ge(deg_done, 1)
            for i in range(NB):
                nc.vector.tensor_scalar(dinv_b[:, i, :], ones[:, :], dinv[:, i:i + 1], None,
                                        ALU.mult).then_inc(dinvb_made, 1)
            link(nc.vector.tensor_scalar(dinv_up[:, :], dinv[:, :], B_UP, None, ALU.mult))
            lo_streamed(0, 0)

            def prepare(u, nth, g):
                for k in range(STREAMED):
                    streamed_moments((u + 1) % 2, nth, k, p_stats)
                variance(0, STREAMED, H_UP, p_stats, g * 3 + 6, p_mv, g + 2, p_ve)

            prepare(0, 0, 0)

            dve.wait_ge(srow_made, 1)
            nc.vector.tensor_scalar(c_row.bitcast(int32), s_row.bitcast(int32), -1, EXPONENT, ALU.bitwise_xor,
                                    ALU.bitwise_and).then_inc(crow_made, 1)

            dve.wait_ge(crow_made, 1)

            def scale_block(i):
                nc.vector.scalar_tensor_tensor(out=a_m[:, i, :], in0=a_m[:, i, :], scalar=dinv_up[:, i:i + 1], in1=c_row,
                                               op0=ALU.mult, op1=ALU.mult).then_inc(b_made, 1)

            scale_block(0)
            for i in range(1, NB, 2):
                scale_block(i)
                if i + 1 < NB:
                    scale_block(i + 1)
                dve.wait_ge(bhi_made, i + 1)
                nc.vector.tensor_tensor(b_lo[:, i, :], a_m[:, i, :], b_hi[:, i, :],
                                        ALU.subtract).then_inc(blo_dve, 1)
            link(nc.vector.tensor_scalar(pow_row.bitcast(int32), s_row.bitcast(int32), EXPONENT, None,
                                         ALU.bitwise_and))
            dve.wait_ge(drow_done, 1)
            nc.vector.scalar_tensor_tensor(out=rs_row[:, :], in0=pow_row, scalar=0.5 / B_UP, in1=big[1],
                                           op0=ALU.mult, op1=ALU.mult).then_inc(rrow_made, 1)
            lo_streamed(1, 1, xwp[0])
            lo_streamed(2, 2)
            dve.wait_ge(bias_loaded, 16)
            dve.wait_ge(rrow_made, 1)

            def finish(it, s, first):
                g, k = it * 2 + s // 4, s % 4
                dve.wait_ge(main_done, g * 4 + (k + 1))
                if not (first and s < 4):
                    dve.wait_ge(out_stored[k], g * 16)
                nc.vector.scalar_tensor_tensor(out=gout[:, k, :], in0=big[k % 2], scalar=w_back[:, 0:1],
                                               in1=rs_row[:, :], op0=ALU.mult, op1=ALU.mult).then_inc(scaled, 1)
                dve.wait_ge(x_loaded[s], it * 16 + (LOADS1 + 16))
                dve.wait_ge(scaled, g * 4 + (k + 1))
                nc.vector.scalar_tensor_tensor(out=gout[:, k, :], in0=gout[:, k, :], scalar=bias_c[:, 0:1],
                                               in1=x1[s], op0=ALU.add, op1=ALU.add).then_inc(out_made, 1)

            def pass2(it, first, last):
                for u in range(2):
                    g = it * 2 + u
                    more = not (last and u == 1)
                    if more:
                        if not (first and u == 0):
                            prepare(u, it if u == 0 else it + 1, g)
                        dve.wait_ge(p_sd, g + 2)
                        nc.vector.reciprocal(y0[:, 0, 0:STREAMED], sd[:, 0, 0:STREAMED]).then_inc(p_y0, 1)
                    for k in range(4):
                        finish(it, 4 * u + k, first)
                        if more and k == 0:
                            for kk in range(STREAMED):
                                low_h(g * 3 + (kk + 3), h32_later[kk], kk)
                        if more and k >= 1:
                            lo_streamed(g * 3 + (k + 2), k - 1)

            pass2(0, True, False)
            with dve.Fori(1, GROUPS // 2 - 1) as it:
                pass2(it, False, False)
            pass2(GROUPS // 2 - 1, False, True)

        @block.tensor
        def _(pe):
            pe.wait_ge(consts, 2)
            pe.wait_ge(w_loaded, 16)
            nc.tensor.transpose(wt_ps, w_in, ident[:, :]).then_inc(w_turned, 1)
            pe.wait_ge(w_scaled, 1)
            nc.tensor.transpose(ws_ps, w_t, ident[:, :]).then_inc(w_back_turned, 1)
            pe.wait_ge(w_ready, 1)

            def make_xw(dst, h_tile, signal):
                for j in range(NB):
                    mm = nc.tensor.matmul(dst[:, j * P:(j + 1) * P], h_tile[:, j * P:(j + 1) * P], w_s[:, :],
                                          start=True, stop=True)
                mm.then_inc(signal, 1)

            def pass1(it, first, last):
                for u in range(4):
                    g = it * 4 + u
                    for k in (2, 3):
                        h_tile = h1[(4 * u + k) % 8]
                        pe.wait_ge(h_made, g * 4 + (k + 1))
                        for c in range(0, N, HALF):
                            mm = nc.tensor.matmul(sum_ps[:, c:c + HALF], ident[:, :], h_tile[:, c:c + HALF],
                                                  start=(first and u == 0 and k == 2),
                                                  stop=(last and u == 3 and k == 3), skip_group_check=True)
                        mm.then_inc(h_used, 1)
                    if not (first and u < 2):
                        pe.wait_ge(lo_made, g - 1)
                    make_xw(xwp[u % 2], h_tile, xw_done)

            pass1(0, True, False)
            with pe.Fori(1, GROUPS // 4 - 1) as it:
                pass1(it, False, False)
            pass1(GROUPS // 4 - 1, False, True)

            def spread(dst, diag, ready, signal):
                pe.wait_ge(ready, 1)
                for j in range(NB):
                    mm = nc.tensor.matmul(dst[:, j * P:(j + 1) * P], ones[:, :], diag[:, j * P:(j + 1) * P],
                                          start=True, stop=True)
                mm.then_inc(signal, 1)

            pe.wait_ge(sq_made, 1)
            for j in range(NB):
                mm = nc.tensor.matmul(norm_ps[:, j:j + 1], x_sq[:, j * P:(j + 1) * P], ones[:, 0:1],
                                      start=True, stop=True)
            mm.then_inc(norm_done, 1)
            spread(big[1], diag_n, diagn_made, rnrow_done)

            pe.wait_ge(xnrm_made, 1)
            for i in range(NB):
                if i >= 2:
                    pe.wait_ge(simh_made, i - 1)
                for c in range(0, N, HALF):
                    mm = nc.tensor.matmul(big[i % 2][:, c:c + HALF], x_nrm[:, i * P:(i + 1) * P],
                                          x_nrm[:, c:c + HALF], start=True, stop=True)
                mm.then_inc(sim_done, 1)

            pe.wait_ge(adj_made, NB)
            pe.wait_ge(simh_made, NB)
            pe.wait_ge(lo_made, GROUPS)
            for i in range(NB):
                if i >= 4:
                    pe.wait_ge(nm_odd if i % 2 else nm_even, i // 2 - 1)
                dst = sym_ps[i % 4]
                for c in range(0, N, HALF):
                    nc.tensor.matmul(dst[:, c:c + HALF], ident16[:, :], adj_m[:, i, c:c + HALF],
                                     start=True, stop=False, skip_group_check=True)
                for j in range(NB):
                    nc.tensor.matmul(dst[:, j * P:(j + 1) * P], adj_m[:, j, i * P:(i + 1) * P], ident16[:, :],
                                     start=False, stop=False, skip_group_check=True)
                nc.tensor.matmul(dst[:, i * P:(i + 1) * P], ident16[:, :], ident16[:, :],
                                 start=False, stop=True, skip_group_check=True).then_inc(sym_done, 1)

            def degree(i):
                pe.wait_ge(alo_pool if i < NB - 1 else alo_dve, i + 1 if i < NB - 1 else 1)
                for part in (a_hi, a_lo):
                    for j in range(NB):
                        mm = nc.tensor.matmul(deg_ps[:, j:j + 1], part[:, i, j * P:(j + 1) * P], ones16[:, 0:1],
                                              start=(i == 0 and j == 0 and part is a_hi),
                                              stop=(i == NB - 1 and part is a_lo), skip_group_check=True)
                return mm

            pe.wait_ge(nm_even, 3)
            for i in range(NB):
                if i >= 2:
                    pe.wait_ge(sq_common, i - 1)
                for kb in range(NB):
                    if i == 0:
                        pe.wait_ge(nm_odd if kb % 2 else nm_even, kb // 2 + 1)
                    for c in range(0, N, HALF):
                        mm = nc.tensor.matmul(big[i % 2][:, c:c + HALF], nm_m[:, kb, i * P:(i + 1) * P],
                                              nm_m[:, kb, c:c + HALF], start=(kb == 0), stop=(kb == NB - 1))
                mm.then_inc(common_done, 1)
                if i >= 3:
                    degree(i - 3)

            def xw_streamed(n, k, n_out, dst=xwp[1]):
                pe.wait_ge(p_hlo, n + 1)
                if n_out is not None:
                    pe.wait_ge(p_lo, n_out)
                pairs = ((0, 0), (0, 1), (1, 0))
                for j in range(NB):
                    for a, b in pairs:
                        mm = nc.tensor.matmul(dst[:, j * P:(j + 1) * P], h16[k][:, a, j * P:(j + 1) * P],
                                              w16[:, b, :], start=((a, b) == pairs[0]), stop=((a, b) == pairs[-1]))
                mm.then_inc(p_xw, 1)

            degree(NB - 3)
            xw_streamed(0, 0, None)
            degree(NB - 2)
            degree(NB - 1).then_inc(deg_done, 1)

            pe.wait_ge(sq_common, NB)
            for i in range(NB):
                pe.wait_ge(dinvb_made, i + 1)
                for c in range(0, N, HALF):
                    mm = nc.tensor.matmul(big[0][:, c:c + HALF], dinv_b[:, i, :], a_hi[:, i, c:c + HALF],
                                          start=(i == 0), stop=(i == NB - 1))
            mm.then_inc(s_done, 1)
            xw_streamed(1, 1, None, xwp[0])
            spread(big[1], diag_d, diagd_made, drow_done)
            xw_streamed(2, 2, 1)

            def node_product(g, k, hi, lo, first):
                dst = big[k % 2]
                for j in range(NB):
                    if first:
                        pe.wait_ge(bhi_made, j + 1)
                        pe.wait_ge(blo_dve if j % 2 else blo_pool, j // 2 + 1)
                    for xw, parts in ((hi, (b_hi, b_lo)), (lo, (b_hi,))):
                        for part in parts:
                            for c in range(0, N, HALF):
                                mm = nc.tensor.matmul(dst[:, c:c + HALF], xw[:, j * P:(j + 1) * P],
                                                      part[:, j, c:c + HALF],
                                                      start=(j == 0 and xw is hi and part is b_hi),
                                                      stop=(j == NB - 1 and xw is lo))
                mm.then_inc(main_done, 1)

            def pass2(it, first, last):
                for u in range(2):
                    g = it * 2 + u
                    for k in range(4):
                        opening = first and u == 0
                        if opening and k < 2:
                            pe.wait_ge(rrow_made if k else srow_made, 1)
                        else:
                            pe.wait_ge(scaled, g * 4 + (k - 1))
                        if k < STREAMED:
                            pe.wait_ge(p_lo, g * 3 + (k + 1))
                            node_product(g, k, xw_u[:, k, 0, :], xw_u[:, k, 1, :], opening and k == 0)
                        else:
                            node_product(g, k, cached_xw(g, 0), cached_xw(g, 1), False)
                        if k >= 1 and not (last and u == 1):
                            xw_streamed(g * 3 + (k + 2), k - 1, g * 3 + (k + 2))

            pass2(0, True, False)
            with pe.Fori(1, GROUPS // 2 - 1) as it:
                pass2(it, False, False)
            pass2(GROUPS // 2 - 1, False, True)


_INS = ['x', 'adj', 'L0_gnn_bias', 'L0_gnn_gumbel']
_OUTS = [((64, 128, 1024), 'float32')]


def kernel(**inputs):
    import numpy as _np
    import concourse.bacc as _bacc
    from concourse import mybir as _mybir
    from concourse.bass_utils import run_bass_kernel_spmd as _run

    nc = _bacc.Bacc("TRN2", target_bir_lowering=False, num_devices=1)
    arrays, args = {}, []
    for name in _INS:
        a = _np.ascontiguousarray(inputs[name])
        arrays[f"in_{name}_dram"] = a
        args.append(nc.dram_tensor(f"in_{name}_dram", a.shape, _mybir.dt.from_np(a.dtype), kind="ExternalInput").ap())
    for i, (shape, dtype) in enumerate(_OUTS):
        dt = _mybir.dt.from_np(_np.dtype(dtype))
        args.append(nc.dram_tensor(f"out_{i}_dram", shape, dt, kind="ExternalOutput").ap())
    bass_preln_graph_layer(nc, *args)
    r = _run(nc, [arrays], core_ids=[0])
    got = tuple(r.results[0][f"out_{i}_dram"] for i in range(len(_OUTS)))
    return got[0]
```

```python
from contextlib import ExitStack

import concourse.bass as bass
from concourse import mybir


def bass_preln_graph_layer(
    nc: bass.Bass,
    x: bass.AP,
    adj: bass.AP,
    bias: bass.AP,
    gumbel: bass.AP,
    out: bass.AP,
):
    fp32 = mybir.dt.float32
    fp16 = mybir.dt.float16
    bf16 = mybir.dt.bfloat16
    int32 = mybir.dt.int32
    ALU = mybir.AluOpType
    ACT = mybir.ActivationFunctionType
    AX = mybir.AxisListType

    B, T, N = x.shape
    P = 128
    NB = N // P
    HALF = 512
    GROUPS = B // 4
    STREAMED = 3
    G_RING = 6
    LN_EPS = 1e-5
    NORM_EPS = 1e-12
    W_TOP = 2.0 ** 9
    H_UP = 2.0 ** 10
    B_UP = 2.0 ** 12
    C_DOWN = 1.0 / 8
    A_ONE = C_DOWN ** 2
    TINY = 1e-18
    EXPONENT = 0x7F800000

    def entry(g, k):
        return g if k == STREAMED else GROUPS + STREAMED * g + k

    SIM_PIECES = ([(0, 0, HALF), (0, HALF, N)] + [(i, 0, N) for i in range(1, NB - 1)]
                  + [(NB - 1, 0, HALF), (NB - 1, HALF, N)])
    PIECES = [(i, 0, N) for i in range(NB - 1)] + [(NB - 1, 0, HALF), (NB - 1, HALF, N)]

    LAST_HALVES = ((0, HALF), (HALF, N))

    gumbel_block = gumbel.rearrange("(i p j) c -> i p (j c)", p=P, j=N)

    ctx = ExitStack()
    with ctx:
        def sb(name, shape, dt=fp32):
            return ctx.enter_context(nc.sbuf_tensor(name, shape, dt))

        def sem(name):
            return ctx.enter_context(nc.semaphore(name))

        cache = sb("cache", [P, GROUPS * 2 * N], fp16)
        xw_u = sb("xw_u", [P, STREAMED, 2, N], fp16)
        xring = sb("xring", [P, 8, N])
        region_a = sb("region_a", [P, 8, N])
        hring = sb("hring", [P, STREAMED, N])
        adj_m = sb("adj_m", [P, NB, N], fp16)
        nm_m = sb("nm_m", [P, NB, N], fp16)
        gout = sb("gout", [P, 4, N])
        rs_row = sb("rs_row", [P, N])

        adj_f = adj_m[:, :, :].rearrange("p a n -> p (a n)").bitcast(fp32)
        nm_f = nm_m[:, :, :].rearrange("p a n -> p (a n)").bitcast(fp32)
        b_hi, b_lo = nm_m, adj_m
        a_m = region_a

        x1 = [xring[:, s, :] for s in range(8)] + [region_a[:, s, :] for s in range(8)]
        h1 = [hring[:, s, :] for s in range(3)] + [adj_f[:, s * N:(s + 1) * N] for s in range(4)] + [nm_f[:, 0:N]]
        pool_sum = nm_f[:, N:2 * N]
        xring_f = xring[:, :, :].rearrange("p a n -> p (a n)")
        goutf = gout[:, :, :].rearrange("p a n -> p (a n)")
        gum = [goutf[:, 0:2 * N], goutf[:, 2 * N:4 * N], nm_f[:, 2 * N:4 * N], xring_f[:, 0:2 * N],
               xring_f[:, 2 * N:4 * N], nm_f[:, 0:2 * N]]
        sim_h = [region_a[:, s, :] for s in (0, 1)]
        one_m = [region_a[:, s, :] for s in (2, 3)]
        score0 = [region_a[:, s, :] for s in (4, 5)]
        score1 = [region_a[:, s, :] for s in (6, 7)]
        x_sum = xring[:, 4, :]
        x_nrm = xring[:, 5, :]
        x_sq = xring[:, 6, :]
        diag_n = xring[:, 7, :]
        xw_uf = xw_u[:, :, :, :].rearrange("p k a n -> p (k a n)").bitcast(fp32)
        c16 = xring[:, 4:8, :].rearrange("p a n -> p (a n)").bitcast(fp16).rearrange(
            "p (a n) -> p a n", n=N)
        a_hi = adj_m
        a_lo = goutf.bitcast(fp16).rearrange("p (a n) -> p a n", n=N)
        h32_first = [xw_uf[:, N:2 * N], xw_uf[:, 2 * N:3 * N], rs_row[:, :]]
        h32_later = [region_a[:, k, :] for k in range(STREAMED)]
        h16 = [hring[:, k, :].bitcast(fp16).rearrange("p (a n) -> p a n", n=N) for k in range(STREAMED)]
        diag_c = gout[:, 1, 0:HALF].bitcast(bf16)
        diag_r = gout[:, 2, :]
        ones_b = gout[:, 3, 0:P // 2].bitcast(bf16)

        w_in = gout[:, 3, 0:P]
        w_t = gout[:, 3, P:2 * P]
        w_s = sb("w_s", [P, P])
        w16 = sb("w16", [P, 2, P], fp16)
        ones16 = sb("ones16", [P, 2], fp16)
        ident = sb("ident", [P, P])
        ident16 = sb("ident16", [P, P], fp16)
        minus16 = sb("minus16", [P, P], fp16)
        ones = sb("ones", [P, P])
        bias_c = sb("bias_c", [P, 1])
        l1 = sb("l1", [P, 1])
        w_pow = sb("w_pow", [P, 1])
        w_up = sb("w_up", [P, 1])
        w_back = sb("w_back", [P, 1])
        stats = sb("stats", [P, 2, 4, 2, 6])
        mv = sb("mv", [P, 2, 4, 2])
        ve4 = sb("ve4", [P, 2, 4])
        sd = sb("sd", [P, 2, 4])
        y0 = sb("y0", [P, 2, 4])
        nt = sb("nt", [P, 2, 4])
        rstd = sb("rstd", [P, 2, 4])
        nmr = sb("nmr", [P, 2, 4])
        threes = sb("threes", [P, 4])
        zeros = sb("zeros", [P, 4])
        wait_pad = sb("wait_pad", [P, 1])
        col_s = sb("col_s", [P, NB])
        col_y = sb("col_y", [P, NB])
        col_t = sb("col_t", [P, NB])
        rnorm = sb("rnorm", [P, NB])
        dinv = sb("dinv", [P, NB])
        dinv_up = sb("dinv_up", [P, NB])
        dinv16 = sb("dinv16", [P, NB], fp16)
        s_col = sb("s_col", [P, NB])
        c_col = sb("c_col", [P, NB])
        r_col = sb("r_col", [P, NB])

        psum = ctx.enter_context(nc.psum_tensor("psum", [P, 8 * HALF], fp32))
        big = [psum[:, 0:N], psum[:, N:2 * N]]
        xwp = [psum[:, 2 * N:3 * N], psum[:, 3 * N:4 * N]]
        sum_ps = big[0]
        wt_ps = big[1][:, 0:P]
        ws_ps = big[1][:, HALF:HALF + P]
        norm_ps = big[1][:, 0:NB]
        deg_ps = xwp[0][:, 0:NB]
        s_ps = xwp[0][:, HALF:HALF + NB]
        c_ps = xwp[0]
        r_ps = xwp[0]
        sym_ps = xwp + big + xwp + xwp

        consts = sem("consts")
        w_loaded = sem("w_loaded")
        bias_loaded = sem("bias_loaded")
        w_turned = sem("w_turned")
        w_scaled = sem("w_scaled")
        w_back_turned = sem("w_back_turned")
        w_ready = sem("w_ready")
        x_loaded = [sem(f"x_loaded{s}") for s in range(16)]
        g_loaded = [sem(f"g_loaded{s}") for s in range(G_RING)]
        dve_step = sem("dve_step")
        pool_step = sem("pool_step")
        stats_made = sem("stats_made")
        mv_made = sem("mv_made")
        ve_made = sem("ve_made")
        sd_made = sem("sd_made")
        y0_made = sem("y0_made")
        rstd_made = sem("rstd_made")
        h_made = sem("h_made")
        h_used = sem("h_used")
        pool_added = sem("pool_added")
        xw_done = sem("xw_done")
        hi_made = sem("hi_made")
        hi_taken = sem("hi_taken")
        lo_dve = sem("lo_dve")
        lo_act = sem("lo_act")
        xsum_made = sem("xsum_made")
        sq_made = sem("sq_made")
        norm_done = sem("norm_done")
        norms_made = sem("norms_made")
        diagn_made = sem("diagn_made")
        rnrow_done = sem("rnrow_done")
        xnrm_made = sem("xnrm_made")
        sim_done = sem("sim_done")
        simh_made = sem("simh_made")
        onem_made = sem("onem_made")
        score0_made = sem("score0_made")
        score1_made = sem("score1_made")
        adj_made = sem("adj_made")
        sym_done = sem("sym_done")
        nm_even = sem("nm_even")
        nm_odd = sem("nm_odd")
        common_done = sem("common_done")
        c16_made = sem("c16_made")
        sq_common = sem("sq_common")
        more_than_one = sem("more_than_one")
        a_made = sem("a_made")
        deg_done = sem("deg_done")
        degs_made = sem("degs_made")
        dinv_made = sem("dinv_made")
        s_done = sem("s_done")
        ahi_made = sem("ahi_made")
        alo_pool = sem("alo_pool")
        alo_dve = sem("alo_dve")
        dinv16_made = sem("dinv16_made")
        onesb_made = sem("onesb_made")
        diagc_made = sem("diagc_made")
        crow_done = sem("crow_done")
        rcol_made = sem("rcol_made")
        diagr_made = sem("diagr_made")
        rrow_done = sem("rrow_done")
        rrow_made = sem("rrow_made")
        b_made = sem("b_made")
        bhi_made = sem("bhi_made")
        blo_dve = sem("blo_dve")
        blo_pool = sem("blo_pool")
        p_stats = sem("p_stats")
        p_mv = sem("p_mv")
        p_ve = sem("p_ve")
        p_sd = sem("p_sd")
        p_y0 = sem("p_y0")
        p_rstd = sem("p_rstd")
        p_h = sem("p_h")
        p_hlo = sem("p_hlo")
        p_hlo_pool = sem("p_hlo_pool")
        p_xw = sem("p_xw")
        p_hi = sem("p_hi")
        p_lo = sem("p_lo")
        main_done = sem("main_done")
        scaled = sem("scaled")
        out_made = sem("out_made")
        out_stored = [sem(f"out_stored{s}") for s in range(4)]

        block = ctx.enter_context(nc.Block())

        def sim_upto(i):
            return sum(1 for piece in SIM_PIECES if piece[0] <= i)

        def halves(tile):
            return tile[:, 0:HALF], tile[:, HALF:N]

        def cached_xw(g, part):
            at = (g * 2 + part) * N
            return cache[:, bass.ds(at, N)]

        @block.sync
        def _(sp):
            def load_x(slot, g, k):
                sp.dma_start(x1[slot], x[entry(g, k), :, :]).then_inc(x_loaded[slot], 16)

            def load_gumbel(i):
                sp.dma_start(gum[i % G_RING], gumbel_block[i, :, :]).then_inc(g_loaded[i % G_RING], 16)

            load_x(0, 0, 0)
            load_x(1, 0, 1)
            sp.dma_start(w_in, adj).then_inc(w_loaded, 16)
            for s in range(2, 16):
                load_x(s, s // 4, s % 4)
            sp.dma_start(bias_c[:, :], bias.rearrange("(p a) -> p a", a=1)).then_inc(bias_loaded, 16)
            with sp.Fori(1, GROUPS // 4) as it:
                for s in range(16):
                    sp.wait_ge(h_made, it * 16 + (s - 15))
                    load_x(s, it * 4 + s // 4, s % 4)

            for i in range(3):
                load_gumbel(i)
            for i, slots in ((3, (0, 1)), (4, (2, 3))):
                for s in slots:
                    sp.wait_ge(h_made, 4 * GROUPS - 15 + s)
                load_gumbel(i)
            sp.wait_ge(xsum_made, 2)
            sp.wait_ge(xw_done, GROUPS)
            load_gumbel(5)
            for i in range(G_RING, NB):
                sp.wait_ge(adj_made, sim_upto(i - G_RING))
                load_gumbel(i)
            for s in range(4):
                if s % 2 == 0:
                    sp.wait_ge(adj_made, sim_upto(3 + s // 2))
                load_x(s, 0, s)
            sp.wait_ge(common_done, len(PIECES))
            for s in range(4, 8):
                load_x(s, 1, s - 4)

            def store(g, k):
                sp.wait_ge(out_made, 4 * g + (k + 1))
                sp.dma_start(out[entry(g, k), :, :], gout[:, k, :]).then_inc(out_stored[k], 16)

            with sp.Fori(0, GROUPS // 2 - 1) as it:
                for s in range(8):
                    store(it * 2 + s // 4, s % 4)
                    load_x(s, it * 2 + (s // 4 + 2), s % 4)
            for s in range(7):
                store(GROUPS - 2 + s // 4, s % 4)
            for h, (c0, c1) in enumerate(LAST_HALVES):
                sp.wait_ge(out_made, B + h)
                sp.dma_start(out[entry(GROUPS - 1, 3), :, c0:c1], gout[:, 3, c0:c1]).then_inc(out_stored[3], 16)
            for k in range(4):
                sp.wait_ge(out_stored[k], 16 * (GROUPS + (1 if k == 3 else 0)))

        @block.gpsimd
        def _(pool):
            step = [0]

            def link(ins):
                step[0] += 1
                ins.then_inc(pool_step, 1)
                pool.wait_ge(pool_step, step[0])

            link(nc.gpsimd.memset(ident[:, :], 0.0))
            link(nc.gpsimd.affine_select(out=ident[:, :], in_=ident[:, :], compare_op=ALU.not_equal, fill=1.0,
                                         base=0, pattern=[[-1, P]], channel_multiplier=1))
            nc.gpsimd.tensor_copy(ident16[:, :], ident[:, :]).then_inc(consts, 1)
            link(nc.gpsimd.memset(ones16[:, :], 1.0))
            link(nc.gpsimd.memset(minus16[:, :], 0.0))
            link(nc.gpsimd.affine_select(out=minus16[:, :], in_=minus16[:, :], compare_op=ALU.not_equal, fill=-1.0,
                                         base=0, pattern=[[-1, P]], channel_multiplier=1))
            nc.gpsimd.memset(ones[:, :], 1.0).then_inc(consts, 1)
            link(nc.gpsimd.memset(threes[:, :], 3.0))
            link(nc.gpsimd.memset(zeros[:, :], 0.0))
            nc.gpsimd.memset(pool_sum, 0.0).then_inc(pool_added, 1)

            def newton(q, kk, y_ready, count, signal, base):
                pool.wait_ge(y_ready, count)
                y, v, t, r, m = y0[:, q, 0:kk], ve4[:, q, 0:kk], nt[:, q, 0:kk], rstd[:, q, 0:kk], nmr[:, q, 0:kk]
                nc.gpsimd.tensor_tensor(t, y, y, ALU.mult).then_inc(pool_step, 1)
                pool.wait_ge(pool_step, base + 1)
                nc.gpsimd.tensor_tensor(t, t, v, ALU.mult).then_inc(pool_step, 1)
                pool.wait_ge(pool_step, base + 2)
                nc.gpsimd.tensor_tensor(t, threes[:, 0:kk], t, ALU.subtract).then_inc(pool_step, 1)
                pool.wait_ge(pool_step, base + 3)
                nc.gpsimd.tensor_tensor(r, y, t, ALU.mult).then_inc(pool_step, 1)
                pool.wait_ge(pool_step, base + 4)
                nc.gpsimd.tensor_tensor(m, mv[:, q, 0:kk, 0], r, ALU.mult).then_inc(pool_step, 1)
                pool.wait_ge(pool_step, base + 5)
                nc.gpsimd.tensor_tensor(m, zeros[:, 0:kk], m, ALU.subtract).then_inc(signal, 1)

            base1 = step[0]
            def add(it, u, k):
                pool.wait_ge(h_made, it * 16 + (4 * u + k + 1))
                pool.wait_ge(pool_added, it * 8 + (2 * u + k + 1))
                nc.gpsimd.tensor_tensor(pool_sum, pool_sum, h1[(4 * u + k) % 8], ALU.add).then_inc(pool_added, 1)

            def pass1(it, first):
                for u in range(4):
                    newton(u % 2, 4, y0_made, it * 4 + (u + 1), rstd_made, it * 20 + (base1 + 5 * u))
                    if not (first and u == 0):
                        add(*((it, u - 1) if u else (it - 1, 3)), 1)
                    add(it, u, 0)

            pass1(0, True)
            with pool.Fori(1, GROUPS // 4) as it:
                pass1(it, False)
            add(GROUPS // 4 - 1, 3, 1)

            for p, (i, c0, c1) in enumerate(SIM_PIECES):
                pool.wait_ge(onem_made, p + 1)
                pool.wait_ge(g_loaded[i % G_RING], 16 * (i // G_RING + 1))
                if i >= 2:
                    pool.wait_ge(adj_made, sim_upto(i - 2))
                nc.gpsimd.tensor_tensor(score1[i % 2][:, c0:c1], one_m[i % 2][:, c0:c1],
                                        gum[i % G_RING][:, 2 * c0 + 1:2 * c1:2], ALU.add).then_inc(score1_made, 1)

            base2 = base1 + 5 * GROUPS
            newton(0, STREAMED, p_y0, 1, p_rstd, base2)
            for i in range(NB - 1):
                pool.wait_ge(ahi_made, i + 1)
                nc.gpsimd.tensor_tensor(a_lo[:, i, :], a_m[:, i, :], a_hi[:, i, :],
                                        ALU.subtract).then_inc(alo_pool, 1)
            pool.wait_ge(deg_done, 1)
            nc.gpsimd.memset(ones_b, 1.0).then_inc(onesb_made, 1)
            pool.wait_ge(p_h, STREAMED)
            nc.gpsimd.tensor_tensor(h16[2][:, 1, :], h32_first[2], h16[2][:, 0, :],
                                    ALU.subtract).then_inc(p_hlo_pool, 1)
            pool.wait_ge(rcol_made, 1)
            for j in range(NB):
                last = nc.gpsimd.tensor_tensor(diag_r[:, j * P:(j + 1) * P], ident[:, :],
                                               r_col[:, j:j + 1].to_broadcast([P, P]), ALU.mult)
            last.then_inc(diagr_made, 1)
            for i in range(0, NB, 2):
                pool.wait_ge(bhi_made, i + 1)
                nc.gpsimd.tensor_tensor(b_lo[:, i, :], a_m[:, i, :], b_hi[:, i, :],
                                        ALU.subtract).then_inc(blo_pool, 1)

            with pool.Fori(1, GROUPS) as g:
                newton(0, STREAMED, p_y0, g + 1, p_rstd, g * 5 + base2)

        @block.scalar
        def _(act):
            def normalise(x_tile, h_tile, q, k, signal):
                ins = nc.scalar.activation(h_tile, x_tile, ACT.Relu, bias=nmr[:, q, k:k + 1],
                                           scale=rstd[:, q, k:k + 1])
                if signal is not None:
                    ins.then_inc(signal, 1)

            def root(q, kk, signal):
                nc.scalar.activation(sd[:, q, 0:kk], ve4[:, q, 0:kk], ACT.Sqrt).then_inc(signal, 1)

            def hi_cached(g, u):
                act.wait_ge(xw_done, g + 1)
                nc.scalar.activation(cached_xw(g, 0), xwp[u], ACT.Copy).then_inc(hi_made, 1)

            def lo_odd(g):
                nc.scalar.activation(cached_xw(g, 1), xwp[1], ACT.Copy).then_inc(lo_act, 1)

            act.wait_ge(ve_made, 1)
            root(0, 4, sd_made)

            def pass1(it, first, last):
                for u in range(4):
                    g = it * 4 + u
                    act.wait_ge(rstd_made, g + 1)
                    for k in range(4):
                        if not (first and u < 2):
                            if k < 2:
                                act.wait_ge(pool_added, g * 2 + (k - 2))
                            else:
                                act.wait_ge(h_used if k == 2 else xw_done, g * 2 - 3 if k == 2 else g - 1)
                        if k == 2 and not (last and u == 3):
                            act.wait_ge(ve_made, g + 2)
                            root((u + 1) % 2, 4, sd_made)
                        if k == 3 and u % 2 == 1 and not (first and u == 1):
                            act.wait_ge(hi_taken, it * 2 + (u - 1) // 2)
                            lo_odd(g - 2)
                        normalise(x1[4 * u + k], h1[(4 * u + k) % 8], u % 2, k, h_made)
                    if not (first and u == 0):
                        hi_cached(g - 1, (u + 1) % 2)

            pass1(0, True, False)
            with act.Fori(1, GROUPS // 4 - 1) as it:
                pass1(it, False, False)
            pass1(GROUPS // 4 - 1, False, True)

            for h in range(2):
                act.wait_ge(xsum_made, h + 1)
                nc.scalar.activation(halves(x_sq)[h], halves(x_sum)[h], ACT.Square).then_inc(sq_made, 1)
            act.wait_ge(norm_done, 1)
            nc.scalar.activation(col_s[:, :], norm_ps, ACT.Sqrt).then_inc(norms_made, 1)
            hi_cached(GROUPS - 1, 1)

            for p, (i, c0, c1) in enumerate(SIM_PIECES):
                act.wait_ge(sim_done, p + 1)
                if i >= 2:
                    act.wait_ge(score0_made, sim_upto(i - 2))
                nc.scalar.activation(sim_h[i % 2][:, c0:c1], big[i % 2][:, c0:c1], ACT.Copy, scale=0.5,
                                     bias=0.5).then_inc(simh_made, 1)
                act.wait_ge(simh_made, p + 1)
                if i >= 2:
                    act.wait_ge(score1_made, sim_upto(i - 2))
                nc.scalar.activation(one_m[i % 2][:, c0:c1], sim_h[i % 2][:, c0:c1], ACT.Copy, scale=-1.0,
                                     bias=1.0).then_inc(onem_made, 1)

            for i in range(0, NB, 2):
                act.wait_ge(sym_done, i + 1)
                nc.scalar.activation(nm_m[:, i, :], sym_ps[i], ACT.Sign).then_inc(nm_even, 1)

            def normalise_streamed(x_tile, h32, k):
                normalise(x_tile, h32, 0, k, None)
                normalise(x_tile, h16[k][:, 0, :], 0, k, p_h)

            def high_a(p):
                i, c0, c1 = PIECES[p]
                act.wait_ge(a_made, p + 1)
                nc.scalar.activation(a_hi[:, i, c0:c1], a_m[:, i, c0:c1], ACT.Copy).then_inc(ahi_made, 1)

            for p, (i, c0, c1) in enumerate(PIECES):
                act.wait_ge(common_done, p + 1)
                act.wait_ge(c16_made, min(i + 1, NB - 1))
                nc.scalar.activation(a_m[:, i, c0:c1], big[i % 2][:, c0:c1], ACT.Square,
                                     scale=C_DOWN).then_inc(sq_common, 1)
                if p >= NB:
                    high_a(p - 1)
                    continue
                if i == 0:
                    act.wait_ge(p_ve, 1)
                    root(0, STREAMED, p_sd)
                if i >= 1:
                    high_a(i - 1)
                    k = (i - 1) // 2
                    if i == 1:
                        act.wait_ge(p_rstd, 1)
                    if i % 2 == 1 and k < STREAMED - 1:
                        normalise(x1[k], h32_first[k], 0, k, None)
                    elif k < STREAMED - 1:
                        normalise(x1[k], h16[k][:, 0, :], 0, k, p_h)
            high_a(len(PIECES) - 1)

            def hi_streamed(n, k, src=xwp[1]):
                act.wait_ge(p_xw, n + 1)
                nc.scalar.activation(xw_u[:, k, 0, :], src, ACT.Copy, scale=1.0 / H_UP).then_inc(p_hi, 1)

            hi_streamed(0, 0)
            act.wait_ge(deg_done, 1)
            nc.scalar.activation(col_s[:, :], deg_ps, ACT.Sqrt).then_inc(degs_made, 1)
            normalise_streamed(x1[2], h32_first[2], 2)
            hi_streamed(1, 1, big[0])
            for i in range(NB):
                act.wait_ge(b_made, i + 1)
                nc.scalar.activation(b_hi[:, i, :], a_m[:, i, :], ACT.Copy).then_inc(bhi_made, 1)
            hi_streamed(2, 2)
            act.wait_ge(rrow_done, 1)
            nc.scalar.activation(rs_row[:, :], r_ps, ACT.Copy).then_inc(rrow_made, 1)

            def pass2(it, us):
                for u in us:
                    g = it * 2 + u
                    act.wait_ge(p_ve, g + 2)
                    root(0, STREAMED, p_sd)
                    act.wait_ge(p_rstd, g + 2)
                    for k in range(STREAMED):
                        act.wait_ge(p_xw, g * 3 + (k + 1))
                        normalise_streamed(x1[4 * ((u + 1) % 2) + k], h32_later[k], k)
                    for k in range(STREAMED):
                        act.wait_ge(main_done, g * 4 + (k + 1))
                        hi_streamed(g * 3 + (k + 3), k)

            with act.Fori(0, GROUPS // 2 - 1) as it:
                pass2(it, (0, 1))
            pass2(GROUPS // 2 - 1, (0,))

        @block.vector
        def _(dve):
            step = [0]

            def link(ins):
                step[0] += 1
                ins.then_inc(dve_step, 1)
                dve.wait_ge(dve_step, step[0])

            def moments(x_tile, q, k, signal):
                nc.vector.bn_stats(stats[:, q, k, 0, :], x_tile[:, 0:HALF])
                nc.vector.bn_stats(stats[:, q, k, 1, :], x_tile[:, HALF:N]).then_inc(signal, 1)

            def variance(q, kk, up, stats_sem, n_stats, mv_sem, n_mv, ve_sem):
                dve.wait_ge(stats_sem, n_stats)
                nc.vector.memset(wait_pad[:, :], 0.0)
                for k in range(kk):
                    last = nc.vector.bn_aggr(mv[:, q, k, :], stats[:, q, k, :, :])
                last.then_inc(mv_sem, 1)
                dve.wait_ge(mv_sem, n_mv)
                nc.vector.tensor_scalar(ve4[:, q, 0:kk], mv[:, q, 0:kk, 1], LN_EPS, 4.0 / up ** 2, ALU.add,
                                        ALU.mult).then_inc(ve_sem, 1)

            def lo_cached(g, u):
                dve.wait_ge(hi_made, g + 1)
                nc.vector.tensor_tensor(cached_xw(g, 1), xwp[u], cached_xw(g, 0), ALU.subtract).then_inc(lo_dve, 1)

            def tile_moments(it, u, k):
                dve.wait_ge(x_loaded[4 * u + k], it * 16 + 16)
                moments(x1[4 * u + k], u % 2, k, stats_made)

            def small(ins):
                step[0] += 1
                ins.then_inc(dve_step, 1)

            def settled():
                dve.wait_ge(dve_step, step[0])

            tile_moments(0, 0, 0)
            tile_moments(0, 0, 1)
            dve.wait_ge(w_turned, 1)
            small(nc.vector.tensor_reduce(l1[:, :], wt_ps, AX.X, ALU.add, apply_absolute_value=True))
            tile_moments(0, 0, 2)
            settled()
            small(nc.vector.tensor_scalar(l1[:, :], l1[:, :], 1e-30, None, ALU.max))
            tile_moments(0, 0, 3)
            settled()
            small(nc.vector.tensor_scalar(w_pow[:, :].bitcast(int32), l1[:, :].bitcast(int32), EXPONENT, None,
                                          ALU.bitwise_and))
            variance(0, 4, 1.0, stats_made, 4, mv_made, 1, ve_made)
            settled()
            small(nc.vector.reciprocal(w_up[:, :], w_pow[:, :]))
            dve.wait_ge(sd_made, 1)
            nc.vector.reciprocal(y0[:, 0, :], sd[:, 0, :]).then_inc(y0_made, 1)
            tile_moments(0, 1, 0)
            settled()
            small(nc.vector.tensor_scalar(w_up[:, :], w_up[:, :], W_TOP, None, ALU.mult))
            small(nc.vector.tensor_scalar(w_back[:, :], w_pow[:, :], 1.0 / W_TOP, None, ALU.mult))
            tile_moments(0, 1, 1)
            settled()
            nc.vector.tensor_scalar(w_t, wt_ps, w_up[:, 0:1], None, ALU.mult).then_inc(w_scaled, 1)
            tile_moments(0, 1, 2)
            dve.wait_ge(w_back_turned, 1)
            small(nc.vector.tensor_copy(w_s[:, :], ws_ps))
            tile_moments(0, 1, 3)
            settled()
            small(nc.vector.tensor_copy(w16[:, 0, :], w_s[:, :]))
            variance(1, 4, 1.0, stats_made, 8, mv_made, 2, ve_made)
            settled()
            nc.vector.tensor_tensor(w16[:, 1, :], w_s[:, :], w16[:, 0, :], ALU.subtract).then_inc(w_ready, 1)

            def pass1(it, first, last):
                for u in range(1 if first else 0, 4):
                    g = it * 4 + u
                    more = not (last and u == 3)
                    nxt = (it, u + 1) if u < 3 else (it + 1, 0)
                    if more:
                        tile_moments(*nxt, 0)
                    dve.wait_ge(sd_made, g + 1)
                    nc.vector.reciprocal(y0[:, u % 2, :], sd[:, u % 2, :]).then_inc(y0_made, 1)
                    if more:
                        for k in range(1, 4):
                            tile_moments(*nxt, k)
                    if u % 2 == 0:
                        lo_cached(g - 2, 0)
                    if more:
                        variance((u + 1) % 2, 4, 1.0, stats_made, g * 4 + 8, mv_made, g + 2, ve_made)

            pass1(0, True, False)
            with dve.Fori(1, GROUPS // 4 - 1) as it:
                pass1(it, False, False)
            pass1(GROUPS // 4 - 1, False, True)

            dve.wait_ge(h_used, 2 * GROUPS)
            dve.wait_ge(pool_added, 2 * GROUPS + 1)
            for h in range(2):
                nc.vector.tensor_tensor(halves(x_sum)[h], halves(sum_ps)[h], halves(pool_sum)[h],
                                        ALU.add).then_inc(xsum_made, 1)

            def refine(v, y):
                link(nc.vector.tensor_tensor(col_t[:, :], y, y, ALU.mult))
                link(nc.vector.tensor_tensor(col_t[:, :], col_t[:, :], v, ALU.mult))
                link(nc.vector.tensor_scalar(col_t[:, :], col_t[:, :], -0.5, 1.5, ALU.mult, ALU.add))
                link(nc.vector.tensor_tensor(y, y, col_t[:, :], ALU.mult))

            dve.wait_ge(norms_made, 1)
            link(nc.vector.tensor_scalar(col_y[:, :], col_s[:, :], TINY, None, ALU.max))
            link(nc.vector.reciprocal(rnorm[:, :], col_y[:, :]))
            refine(norm_ps, rnorm[:, :])
            link(nc.vector.tensor_scalar(rnorm[:, :], rnorm[:, :], 1.0 / (B * NORM_EPS), None, ALU.min))
            for j in range(NB):
                nc.vector.tensor_scalar(diag_n[:, j * P:(j + 1) * P], ident[:, :], rnorm[:, j:j + 1], None,
                                        ALU.mult).then_inc(diagn_made, 1)
            dve.wait_ge(xsum_made, 2)
            for h in range(2):
                dve.wait_ge(rnrow_done, h + 1)
                nc.vector.tensor_tensor(halves(x_nrm)[h], halves(x_sum)[h], halves(big[1])[h],
                                        ALU.mult).then_inc(xnrm_made, 1)
            lo_cached(GROUPS - 2, 0)
            lo_cached(GROUPS - 1, 1)

            def make_score0(p):
                i, c0, c1 = SIM_PIECES[p]
                dve.wait_ge(simh_made, p + 1)
                dve.wait_ge(g_loaded[i % G_RING], 16 * (i // G_RING + 1))
                if i >= 2:
                    dve.wait_ge(adj_made, sim_upto(i - 2))
                nc.vector.tensor_tensor(score0[i % 2][:, c0:c1], sim_h[i % 2][:, c0:c1],
                                        gum[i % G_RING][:, 2 * c0:2 * c1:2], ALU.add).then_inc(score0_made, 1)

            make_score0(0)
            for p, (i, c0, c1) in enumerate(SIM_PIECES):
                if p + 1 < len(SIM_PIECES):
                    make_score0(p + 1)
                dve.wait_ge(score1_made, p + 1)
                dve.wait_ge(score0_made, p + 1)
                nc.vector.tensor_tensor(adj_m[:, i, c0:c1], score0[i % 2][:, c0:c1], score1[i % 2][:, c0:c1],
                                        ALU.is_gt).then_inc(adj_made, 1)

            for i in range(1, NB, 2):
                dve.wait_ge(sym_done, i + 1)
                nc.vector.tensor_scalar(nm_m[:, i, :], sym_ps[i], 1.0, None, ALU.min).then_inc(nm_odd, 1)

            LOADS1 = 16 * (GROUPS // 4)

            def streamed_moments(q, nth, k, signal):
                dve.wait_ge(x_loaded[4 * q + k], nth * 16 + (LOADS1 + 16))
                moments(x1[4 * q + k], 0, k, signal)

            def low_h(n, h32, k):
                dve.wait_ge(p_h, n + 1)
                nc.vector.tensor_tensor(h16[k][:, 1, :], h32, h16[k][:, 0, :], ALU.subtract).then_inc(p_hlo, 1)

            def low_a(p):
                i, c0, c1 = PIECES[p]
                dve.wait_ge(ahi_made, p + 1)
                nc.vector.tensor_tensor(a_lo[:, i, c0:c1], a_m[:, i, c0:c1], a_hi[:, i, c0:c1],
                                        ALU.subtract).then_inc(alo_dve, 1)

            def keep_common(i):
                dve.wait_ge(common_done, i + 1)
                nc.vector.tensor_copy(c16[:, i, (i + 1) * P:N], big[i % 2][:, (i + 1) * P:N]).then_inc(c16_made, 1)

            streamed_moments(0, 0, 0, p_stats)
            streamed_moments(0, 0, 1, p_stats)
            keep_common(0)
            streamed_moments(0, 0, 2, p_stats)
            variance(0, STREAMED, H_UP, p_stats, STREAMED, p_mv, 1, p_ve)
            for p, (i, c0, c1) in enumerate(PIECES):
                if i + 1 < NB - 1:
                    keep_common(i + 1)
                dve.wait_ge(sq_common, p + 1)
                if c0 <= i * P < c1:
                    on_diag = a_m[:, i, i * P:(i + 1) * P]
                    nc.vector.scalar_tensor_tensor(out=on_diag, in0=on_diag, scalar=A_ONE, in1=on_diag,
                                                   op0=ALU.is_gt, op1=ALU.mult).then_inc(more_than_one, 1)
                    dve.wait_ge(more_than_one, i + 1)
                nc.vector.tensor_tensor(a_m[:, i, c0:c1], a_m[:, i, c0:c1], adj_m[:, i, c0:c1],
                                        ALU.mult).then_inc(a_made, 1)
                if i == 0:
                    dve.wait_ge(p_sd, 1)
                    nc.vector.reciprocal(y0[:, 0, 0:STREAMED], sd[:, 0, 0:STREAMED]).then_inc(p_y0, 1)
                if i in (2, 4):
                    low_h(i // 2 - 1, h32_first[i // 2 - 1], i // 2 - 1)
            low_a(NB - 1)
            low_a(NB)

            dve.wait_ge(degs_made, 1)
            link(nc.vector.tensor_scalar(col_y[:, :], col_s[:, :], TINY, None, ALU.max))
            link(nc.vector.reciprocal(dinv[:, :], col_y[:, :]))
            refine(deg_ps, dinv[:, :])
            nc.vector.scalar_tensor_tensor(out=dinv[:, :], in0=deg_ps, scalar=0.0, in1=dinv[:, :],
                                           op0=ALU.is_gt, op1=ALU.mult).then_inc(dinv_made, 1)

            def lo_streamed(n, k, src=xwp[1]):
                dve.wait_ge(p_hi, n + 1)
                nc.vector.scalar_tensor_tensor(out=xw_u[:, k, 1, :], in0=src, scalar=1.0 / H_UP,
                                               in1=xw_u[:, k, 0, :], op0=ALU.mult, op1=ALU.subtract).then_inc(p_lo, 1)

            dve.wait_ge(dinv_made, 1)
            nc.vector.tensor_copy(dinv16[:, :], dinv[:, :]).then_inc(dinv16_made, 1)
            link(nc.vector.tensor_scalar(dinv_up[:, :], dinv[:, :], B_UP, None, ALU.mult))
            lo_streamed(0, 0)

            def prepare(u, nth, g):
                for k in range(STREAMED):
                    streamed_moments((u + 1) % 2, nth, k, p_stats)
                variance(0, STREAMED, H_UP, p_stats, g * 3 + 6, p_mv, g + 2, p_ve)

            dve.wait_ge(s_done, 1)
            link(nc.vector.tensor_scalar(s_col[:, :], s_ps, 1e-20, None, ALU.max))
            link(nc.vector.tensor_scalar(c_col[:, :].bitcast(int32), s_col[:, :].bitcast(int32), -1, EXPONENT,
                                         ALU.bitwise_xor, ALU.bitwise_and))
            for j in range(NB):
                nc.vector.tensor_scalar(diag_c[:, j * P:(j + 1) * P], ident[:, :], c_col[:, j:j + 1], None,
                                        ALU.mult).then_inc(diagc_made, 1)
            link(nc.vector.tensor_scalar(r_col[:, :].bitcast(int32), s_col[:, :].bitcast(int32), EXPONENT, None,
                                         ALU.bitwise_and))
            nc.vector.scalar_tensor_tensor(out=r_col[:, :], in0=r_col[:, :], scalar=0.5 / B_UP, in1=dinv[:, :],
                                           op0=ALU.mult, op1=ALU.mult).then_inc(rcol_made, 1)

            dve.wait_ge(crow_done, 1)
            for i in range(NB):
                nc.vector.scalar_tensor_tensor(out=a_m[:, i, :], in0=a_m[:, i, :], scalar=dinv_up[:, i:i + 1], in1=c_ps,
                                               op0=ALU.mult, op1=ALU.mult).then_inc(b_made, 1)
                if i == 0:
                    lo_streamed(1, 1, big[0])
            for i in range(1, NB, 2):
                dve.wait_ge(bhi_made, i + 1)
                nc.vector.tensor_tensor(b_lo[:, i, :], a_m[:, i, :], b_hi[:, i, :],
                                        ALU.subtract).then_inc(blo_dve, 1)
            prepare(0, 0, 0)
            lo_streamed(2, 2)
            dve.wait_ge(bias_loaded, 16)
            dve.wait_ge(rrow_made, 1)

            def finish(it, s, first, c0=0, c1=N, h=0):
                g, k = it * 2 + s // 4, s % 4
                dve.wait_ge(main_done, g * 4 + (k + 1 + h))
                if not (first and s < 4):
                    dve.wait_ge(out_stored[k], g * 16)
                nc.vector.scalar_tensor_tensor(out=gout[:, k, c0:c1], in0=big[k % 2][:, c0:c1], scalar=w_back[:, 0:1],
                                               in1=rs_row[:, c0:c1], op0=ALU.mult, op1=ALU.mult).then_inc(scaled, 1)
                dve.wait_ge(x_loaded[s], it * 16 + (LOADS1 + 16))
                dve.wait_ge(scaled, g * 4 + (k + 1 + h))
                nc.vector.scalar_tensor_tensor(out=gout[:, k, c0:c1], in0=gout[:, k, c0:c1], scalar=bias_c[:, 0:1],
                                               in1=x1[s][:, c0:c1], op0=ALU.add, op1=ALU.add).then_inc(out_made, 1)

            def pass2(it, first, last):
                for u in range(2):
                    g = it * 2 + u
                    more = not (last and u == 1)
                    if more:
                        if not (first and u == 0):
                            prepare(u, it if u == 0 else it + 1, g)
                        dve.wait_ge(p_sd, g + 2)
                        nc.vector.reciprocal(y0[:, 0, 0:STREAMED], sd[:, 0, 0:STREAMED]).then_inc(p_y0, 1)
                    for k in range(4 if more else 3):
                        finish(it, 4 * u + k, first)
                        if more and k == 0:
                            for kk in range(STREAMED):
                                low_h(g * 3 + (kk + 3), h32_later[kk], kk)
                        if more and k >= 1:
                            lo_streamed(g * 3 + (k + 2), k - 1)

            pass2(0, True, False)
            with dve.Fori(1, GROUPS // 2 - 1) as it:
                pass2(it, False, False)
            pass2(GROUPS // 2 - 1, False, True)
            for h, (c0, c1) in enumerate(LAST_HALVES):
                finish(GROUPS // 2 - 1, 7, False, c0, c1, h)

        @block.tensor
        def _(pe):
            pe.wait_ge(consts, 2)
            pe.wait_ge(w_loaded, 16)
            nc.tensor.transpose(wt_ps, w_in, ident[:, :]).then_inc(w_turned, 1)
            pe.wait_ge(w_scaled, 1)
            nc.tensor.transpose(ws_ps, w_t, ident[:, :]).then_inc(w_back_turned, 1)

            def make_xw(dst, h_tile, signal):
                for j in range(NB):
                    mm = nc.tensor.matmul(dst[:, j * P:(j + 1) * P], h_tile[:, j * P:(j + 1) * P], w_s[:, :],
                                          start=(j * P % HALF == 0), stop=False, skip_group_check=True)
                mm.then_inc(signal, 1)

            def pass1(it, first, last):
                for u in range(4):
                    g = it * 4 + u
                    for k in (2, 3):
                        h_tile = h1[(4 * u + k) % 8]
                        pe.wait_ge(h_made, g * 4 + (k + 1))
                        for c in range(0, N, HALF):
                            mm = nc.tensor.matmul(sum_ps[:, c:c + HALF], ident[:, :], h_tile[:, c:c + HALF],
                                                  start=(first and u == 0 and k == 2),
                                                  stop=(last and u == 3 and k == 3), skip_group_check=True)
                        mm.then_inc(h_used, 1)
                    if u % 2 == 0 and not (first and u == 0):
                        pe.wait_ge(hi_made, g)
                        for c in range(0, N, HALF):
                            mm = nc.tensor.matmul(xwp[1][:, c:c + HALF], minus16[:, :],
                                                  cached_xw(g - 1, 0)[:, c:c + HALF],
                                                  start=False, stop=True, skip_group_check=True)
                        mm.then_inc(hi_taken, 1)
                    if not (first and u < 2):
                        pe.wait_ge(lo_act if u % 2 else lo_dve, it * 2 + u // 2)
                    if first and u == 0:
                        pe.wait_ge(w_ready, 1)
                    if not (last and u == 3):
                        make_xw(xwp[u % 2], h_tile, xw_done)

            pass1(0, True, False)
            with pe.Fori(1, GROUPS // 4 - 1) as it:
                pass1(it, False, False)
            pass1(GROUPS // 4 - 1, False, True)

            for j in range(NB):
                if j * P % HALF == 0:
                    pe.wait_ge(sq_made, j * P // HALF + 1)
                mm = nc.tensor.matmul(norm_ps[:, j:j + 1], x_sq[:, j * P:(j + 1) * P], ones[:, 0:1],
                                      start=True, stop=True)
            mm.then_inc(norm_done, 1)
            make_xw(xwp[1], h1[7], xw_done)
            for j in range(NB):
                pe.wait_ge(diagn_made, j + 1)
                mm = nc.tensor.matmul(big[1][:, j * P:(j + 1) * P], ones[:, :], diag_n[:, j * P:(j + 1) * P],
                                      start=True, stop=True)
                if (j + 1) * P % HALF == 0:
                    mm.then_inc(rnrow_done, 1)

            def own_rows(i):
                for c in range(0, N, HALF):
                    nc.tensor.matmul(sym_ps[i][:, c:c + HALF], ident16[:, :], adj_m[:, i, c:c + HALF],
                                     start=True, stop=False, skip_group_check=True)

            def turned(i, j):
                nc.tensor.matmul(sym_ps[i][:, j * P:(j + 1) * P], adj_m[:, j, i * P:(i + 1) * P], ident16[:, :],
                                 start=False, stop=False, skip_group_check=True)

            def own_node(i):
                nc.tensor.matmul(sym_ps[i][:, i * P:(i + 1) * P], ident16[:, :], ident16[:, :],
                                 start=False, stop=True, skip_group_check=True).then_inc(sym_done, 1)

            def sym_follow(rows, j):
                pe.wait_ge(adj_made, sim_upto(j) if j < NB - 1 else sim_upto(j) - 1)
                for i in rows:
                    if j >= i:
                        if j == i:
                            own_rows(i)
                        for jj in range(j + 1) if j == i else (j,):
                            turned(i, jj)

            for i, c0, c1 in SIM_PIECES:
                if i >= 2:
                    pe.wait_ge(simh_made, sim_upto(i - 2))
                for c in range(c0, c1, HALF):
                    if i == 0:
                        pe.wait_ge(xnrm_made, c // HALF + 1)
                    mm = nc.tensor.matmul(big[i % 2][:, c:c + HALF], x_nrm[:, i * P:(i + 1) * P],
                                          x_nrm[:, c:c + HALF], start=True, stop=True)
                mm.then_inc(sim_done, 1)
                if i >= 3 and c1 == N:
                    if i == 3:
                        pe.wait_ge(lo_dve, GROUPS // 2 + 1)
                    sym_follow((0, 1), i - 3)
            pe.wait_ge(simh_made, sim_upto(NB - 1))
            for j in range(NB - 1):
                sym_follow((2, 3), j)
                if j > NB - 4:
                    sym_follow((0, 1), j)
            sym_follow((0, 1, 2, 3), NB - 1)
            for i in range(4):
                own_node(i)
            pe.wait_ge(adj_made, sim_upto(NB - 1))
            for i in range(4, NB):
                pe.wait_ge(nm_odd if i % 2 else nm_even, 1 if i < 6 else 3)
                own_rows(i)
                for j in range(NB):
                    turned(i, j)
                own_node(i)

            def degree(p):
                i, c0, c1 = PIECES[p]
                pe.wait_ge(alo_pool if i < NB - 1 else alo_dve, i + 1 if i < NB - 1 else p - (NB - 2))
                for part in (a_hi, a_lo):
                    for j in range(c0 // P, c1 // P):
                        mm = nc.tensor.matmul(deg_ps[:, j:j + 1], part[:, i, j * P:(j + 1) * P], ones16[:, 0:1],
                                              start=(i == 0 and j == 0 and part is a_hi),
                                              stop=(i == NB - 1 and part is a_lo), skip_group_check=True)
                return mm

            for i, c0, c1 in PIECES:
                dst = big[i % 2]
                banks = range(c0, c1, HALF)
                if i >= 2:
                    pe.wait_ge(sq_common, i - 1)
                for kb in range(NB):
                    if i == 0:
                        pe.wait_ge(nm_odd if kb % 2 else nm_even, kb // 2 + 1)
                    for c in banks:
                        left = max(c, i * P)
                        if left < c + HALF:
                            mm = nc.tensor.matmul(dst[:, left:c + HALF], nm_m[:, kb, i * P:(i + 1) * P],
                                                  nm_m[:, kb, left:c + HALF], start=(kb == 0), stop=(kb == NB - 1),
                                                  skip_group_check=True)
                if i >= 1:
                    pe.wait_ge(c16_made, i)
                for j in range(c0 // P, min(i, c1 // P)):
                    mm = nc.tensor.matmul(dst[:, j * P:(j + 1) * P], c16[:, j, i * P:(i + 1) * P], ident16[:, :],
                                          start=(j * P % HALF == 0 and i * P >= (j + 4) * P), stop=True,
                                          skip_group_check=True)
                mm.then_inc(common_done, 1)
                if i >= 4 and c0 == 0:
                    degree(i - 4)

            def xw_streamed(k, n_out, dst=xwp[1]):
                if n_out is not None:
                    pe.wait_ge(p_lo, n_out)
                pairs = ((0, 0), (0, 1), (1, 0))
                for j in range(NB):
                    for a, b in pairs:
                        mm = nc.tensor.matmul(dst[:, j * P:(j + 1) * P], h16[k][:, a, j * P:(j + 1) * P],
                                              w16[:, b, :], start=((a, b) == pairs[0]), stop=((a, b) == pairs[-1]))
                mm.then_inc(p_xw, 1)

            pe.wait_ge(p_hlo, 1)
            xw_streamed(0, None)
            degree(NB - 4)
            degree(NB - 3)
            degree(NB - 2)
            degree(NB - 1)
            degree(NB).then_inc(deg_done, 1)

            pe.wait_ge(sq_common, NB + 1)
            pe.wait_ge(p_hlo, 2)
            xw_streamed(1, None, big[0])

            pe.wait_ge(dinv16_made, 1)
            for j in range(NB):
                for i in range(NB):
                    mm = nc.tensor.matmul(s_ps[:, j:j + 1], a_hi[:, i, j * P:(j + 1) * P], dinv16[:, i:i + 1],
                                          start=(i == 0), stop=(i == NB - 1))
            mm.then_inc(s_done, 1)

            pe.wait_ge(onesb_made, 1)
            for j in range(NB):
                pe.wait_ge(diagc_made, j + 1)
                mm = nc.tensor.matmul(c_ps[:, j * P:(j + 1) * P], ones_b, diag_c[:, j * P:(j + 1) * P],
                                      start=True, stop=True)
            mm.then_inc(crow_done, 1)
            pe.wait_ge(p_hlo_pool, 1)
            xw_streamed(2, 1)

            pe.wait_ge(p_lo, 2)
            for j in range(NB):
                pe.wait_ge(bhi_made, j + 1)
                for k in (0, 1):
                    for part in (0, 1):
                        for c in range(0, N, HALF):
                            nc.tensor.matmul(big[k][:, c:c + HALF], xw_u[:, k, part, j * P:(j + 1) * P],
                                             b_hi[:, j, c:c + HALF], start=(j == 0 and part == 0), stop=False)
                if j == NB - 3:
                    pe.wait_ge(b_made, NB)
                    pe.wait_ge(diagr_made, 1)
                    for d in range(NB):
                        mm = nc.tensor.matmul(r_ps[:, d * P:(d + 1) * P], ones[:, :], diag_r[:, d * P:(d + 1) * P],
                                              start=True, stop=True)
                    mm.then_inc(rrow_done, 1)
            for k in (0, 1):
                for j in range(NB):
                    if k == 0:
                        pe.wait_ge(blo_dve if j % 2 else blo_pool, j // 2 + 1)
                    for c in range(0, N, HALF):
                        mm = nc.tensor.matmul(big[k][:, c:c + HALF], xw_u[:, k, 0, j * P:(j + 1) * P],
                                              b_lo[:, j, c:c + HALF], start=False, stop=(j == NB - 1))
                mm.then_inc(main_done, 1)

            def node_product(k, hi, lo, c0=0, c1=N):
                dst = big[k % 2]
                for j in range(NB):
                    for xw, parts in ((hi, (b_hi, b_lo)), (lo, (b_hi,))):
                        for part in parts:
                            for c in range(c0, c1, HALF):
                                mm = nc.tensor.matmul(dst[:, c:c + HALF], xw[:, j * P:(j + 1) * P],
                                                      part[:, j, c:c + HALF],
                                                      start=(j == 0 and xw is hi and part is b_hi),
                                                      stop=(j == NB - 1 and xw is lo))
                mm.then_inc(main_done, 1)

            def pass2(it, first, last):
                for u in range(2):
                    g = it * 2 + u
                    for k in range(4):
                        if not (first and u == 0 and k < 2):
                            pe.wait_ge(scaled, g * 4 + (k - 1))
                            if k < STREAMED:
                                pe.wait_ge(p_lo, g * 3 + (k + 1))
                                node_product(k, xw_u[:, k, 0, :], xw_u[:, k, 1, :])
                            else:
                                for c0, c1 in LAST_HALVES if last and u == 1 else ((0, N),):
                                    node_product(k, cached_xw(g, 0), cached_xw(g, 1), c0, c1)
                        if k >= 1 and not (last and u == 1):
                            pe.wait_ge(p_hlo, g * 3 + (k + 2))
                            xw_streamed(k - 1, g * 3 + (k + 2))

            pass2(0, True, False)
            with pe.Fori(1, GROUPS // 2 - 1) as it:
                pass2(it, False, False)
            pass2(GROUPS // 2 - 1, False, True)


_INS = ['x', 'adj', 'L0_gnn_bias', 'L0_gnn_gumbel']
_OUTS = [((64, 128, 1024), 'float32')]


def kernel(**inputs):
    import numpy as _np
    import concourse.bacc as _bacc
    from concourse import mybir as _mybir
    from concourse.bass_utils import run_bass_kernel_spmd as _run

    nc = _bacc.Bacc("TRN2", target_bir_lowering=False, num_devices=1)
    arrays, args = {}, []
    for name in _INS:
        a = _np.ascontiguousarray(inputs[name])
        arrays[f"in_{name}_dram"] = a
        args.append(nc.dram_tensor(f"in_{name}_dram", a.shape, _mybir.dt.from_np(a.dtype), kind="ExternalInput").ap())
    for i, (shape, dtype) in enumerate(_OUTS):
        dt = _mybir.dt.from_np(_np.dtype(dtype))
        args.append(nc.dram_tensor(f"out_{i}_dram", shape, dt, kind="ExternalOutput").ap())
    bass_preln_graph_layer(nc, *args)
    r = _run(nc, [arrays], core_ids=[0])
    got = tuple(r.results[0][f"out_{i}_dram"] for i in range(len(_OUTS)))
    return got[0]
```
